# Optimizing a Trainium2 kernel written in Bass

```python
import numpy as np
import jax
import jax.numpy as jnp

def _softmax(x, axis=-1):
    return jax.nn.softmax(x, axis=axis)

def _gelu(x):
    return jax.nn.gelu(x, approximate=True)

def _silu(x):
    return jax.nn.silu(x)

def _sigmoid(x):
    return jax.nn.sigmoid(x)

def _layernorm(x, axis=-1, eps=1e-05):
    m = jnp.mean(x, axis=axis, keepdims=True)
    v = jnp.var(x, axis=axis, keepdims=True)
    return (x - m) / jnp.sqrt(v + eps)

def _scatter_add(tgt, idx, src, axis=0):
    return tgt.at[idx].add(src)

def _segment_sum(src, seg, n):
    return jax.ops.segment_sum(src, seg, n)
kernel_name = 'mk_metaformer_d1_conv_nhwc256_r2_f0bee3'

def setup_inputs(seed: int=0):
    np.random.seed(seed)
    _w = jnp.asarray

    def _rec_inputs():
        import jax
        import jax.numpy as jnp
        _gk = jax.random.key(seed)
        x = -0.0005153 + 1.001 * jax.random.normal(jax.random.fold_in(_gk, 1), (4, 56, 56, 128), jnp.float32)
        return x
    x = _rec_inputs()

    def _L0_conv_setup():
        import jax, jax.numpy as jnp
        import numpy as np
        K = 7
        G = 16
        BN_EPS = 0.001
        key = jax.random.key(seed)
        ks = jax.random.split(key, 6)
        B, H, W, C = (4, 56, 56, 128)
        Cr = C // 4
        x = jax.random.normal(ks[0], (B, H, W, C), dtype=jnp.float32)
        w_reduce = jax.random.normal(ks[1], (C, Cr), dtype=jnp.float32) * (1.0 / np.sqrt(C))
        gamma = jnp.ones((Cr,), dtype=jnp.float32)
        beta = jnp.zeros((Cr,), dtype=jnp.float32)
        mean = jax.random.normal(ks[2], (Cr,), dtype=jnp.float32) * 0.1
        var = jax.random.uniform(ks[3], (Cr,), dtype=jnp.float32) + 0.5
        w_span = jax.random.normal(ks[4], (Cr, K * K * G), dtype=jnp.float32) * (1.0 / np.sqrt(Cr))
        b_span = jnp.zeros((K * K * G,), dtype=jnp.float32)
        return {'x': x, 'w_reduce': w_reduce, 'gamma': gamma, 'beta': beta, 'mean': mean, 'var': var, 'w_span': w_span, 'b_span': b_span}
    _L0_conv_all = _L0_conv_setup()
    _L0_conv_in = {k: v for k, v in _L0_conv_all.items() if k in ('w_reduce', 'gamma', 'beta', 'mean', 'var', 'w_span', 'b_span')}
    del _L0_conv_all

    def _L0_ffn_setup():
        import jax, jax.numpy as jnp
        import numpy as np
        B, T, D, H, E = (16, 2048, 128, 256, 8)
        key = jax.random.key(seed)
        ks = jax.random.split(key, 5)
        x = jax.random.normal(ks[0], (B, T, D), dtype=jnp.float32)
        gate_w = jax.random.normal(ks[1], (D, E), dtype=jnp.float32) * 0.02
        gate_b = jnp.zeros((E,), dtype=jnp.float32)
        W1 = jax.random.normal(ks[2], (E, D, H), dtype=jnp.float32) * 0.02
        b1 = jnp.zeros((E, H), dtype=jnp.float32)
        W2 = jax.random.normal(ks[3], (E, H, D), dtype=jnp.float32) * 0.02
        b2 = jnp.zeros((E, D), dtype=jnp.float32)
        return {'x': x, 'gate_w': gate_w, 'gate_b': gate_b, 'W1': W1, 'b1': b1, 'W2': W2, 'b2': b2}
    _L0_ffn_all = _L0_ffn_setup()
    _L0_ffn_in = {k: v for k, v in _L0_ffn_all.items() if k in ('gate_w', 'gate_b', 'W1', 'b1', 'W2', 'b2')}
    del _L0_ffn_all
    return {'x': x, 'L0_conv_w_reduce': _L0_conv_in['w_reduce'], 'L0_conv_gamma': _L0_conv_in['gamma'], 'L0_conv_beta': _L0_conv_in['beta'], 'L0_conv_mean': _L0_conv_in['mean'], 'L0_conv_var': _L0_conv_in['var'], 'L0_conv_w_span': _L0_conv_in['w_span'], 'L0_conv_b_span': _L0_conv_in['b_span'], 'L0_ffn_gate_w': _L0_ffn_in['gate_w'], 'L0_ffn_gate_b': _L0_ffn_in['gate_b'], 'L0_ffn_W1': _L0_ffn_in['W1'], 'L0_ffn_b1': _L0_ffn_in['b1'], 'L0_ffn_W2': _L0_ffn_in['W2'], 'L0_ffn_b2': _L0_ffn_in['b2']}

def reference(x, L0_conv_w_reduce, L0_conv_gamma, L0_conv_beta, L0_conv_mean, L0_conv_var, L0_conv_w_span, L0_conv_b_span, L0_ffn_gate_w, L0_ffn_gate_b, L0_ffn_W1, L0_ffn_b1, L0_ffn_W2, L0_ffn_b2):
    import jax
    import jax.numpy as jnp

    def _L0_conv_ref(x, w_reduce, gamma, beta, mean, var, w_span, b_span):
        import jax, jax.numpy as jnp
        import numpy as np
        K = 7
        G = 16
        BN_EPS = 0.001
        B, H, W, C = x.shape
        Cg = C // G
        r = jnp.einsum('bhwc,cd->bhwd', x, w_reduce)
        r = jax.nn.relu((r - mean) * (gamma / jnp.sqrt(var + BN_EPS)) + beta)
        kgen = jnp.einsum('bhwd,de->bhwe', r, w_span) + b_span
        kgen = kgen.reshape(B, H, W, G, K * K)
        p = (K - 1) // 2
        xp = jnp.pad(x, ((0, 0), (p, p), (p, p), (0, 0)))
        patches = jnp.stack([xp[:, i:i + H, j:j + W, :] for i in range(K) for j in range(K)], axis=3)
        patches = patches.reshape(B, H, W, K * K, G, Cg)
        out = jnp.einsum('bhwgk,bhwkgc->bhwgc', kgen, patches)
        return out.reshape(B, H, W, C)

    def _L0_ffn_ref(x, gate_w, gate_b, W1, b1, W2, b2):
        import jax, jax.numpy as jnp
        import numpy as np
        B, T, D, H, E = (16, 2048, 128, 256, 8)
        Bb, Tt, Dd = x.shape
        Ee = gate_w.shape[1]
        xf = x.reshape(-1, Dd)
        N = xf.shape[0]
        logits = xf @ gate_w + gate_b
        probs = jax.nn.softmax(logits, axis=-1)
        top2_vals, top2_idx = jax.lax.top_k(probs, 2)
        cw = jnp.zeros((N, Ee), dtype=xf.dtype).at[jnp.arange(N)[:, None], top2_idx].add(top2_vals)

        def step(acc, params):
            w1, bb1, w2, bb2, we = params
            h = jax.nn.gelu(xf @ w1 + bb1, approximate=False)
            y = h @ w2 + bb2
            return (acc + we[:, None] * y, None)
        out, _ = jax.lax.scan(step, jnp.zeros_like(xf), (W1, b1, W2, b2, cw.T))
        return out.reshape(Bb, Tt, Dd)

    def _gn(v, G=32, eps=1e-05):
        B_, H_, W_, C_ = v.shape
        g = v.reshape(B_, H_, W_, G, C_ // G)
        m = jnp.mean(g, axis=(1, 2, 4), keepdims=True)
        s = jnp.var(g, axis=(1, 2, 4), keepdims=True)
        return ((g - m) / jnp.sqrt(s + eps)).reshape(v.shape)

    def _ln_c(v, eps=1e-06):
        m = jnp.mean(v, axis=-1, keepdims=True)
        s = jnp.var(v, axis=-1, keepdims=True)
        return (v - m) / jnp.sqrt(s + eps)

    def _ln_t(v, eps=1e-05):
        m = jnp.mean(v, axis=-1, keepdims=True)
        s = jnp.var(v, axis=-1, keepdims=True)
        return (v - m) / jnp.sqrt(s + eps)

    def _to_tokens(v):
        B_, H_, W_, C_ = v.shape
        return v.reshape(B_, H_ * W_, C_)

    def _from_tokens(t, like):
        return t.reshape(like.shape)
    x = x + _L0_conv_ref(_ln_c(x), L0_conv_w_reduce, L0_conv_gamma, L0_conv_beta, L0_conv_mean, L0_conv_var, L0_conv_w_span, L0_conv_b_span)
    t = _to_tokens(x)
    t = t + _L0_ffn_ref(_ln_t(t), L0_ffn_gate_w, L0_ffn_gate_b, L0_ffn_W1, L0_ffn_b1, L0_ffn_W2, L0_ffn_b2)
    x = _from_tokens(t, x)
    return x

_drawn_inputs = setup_inputs


def setup_inputs(seed=0):
    import zlib

    import numpy as np

    out = dict(_drawn_inputs(seed))
    spreads = {'L0_conv_gamma': (1.0, 0.2),
     'L0_conv_beta': (0.0, 0.1),
     'L0_conv_b_span': (0.0, 0.1),
     'L0_ffn_gate_b': (0.0, 0.8),
     'L0_ffn_b1': (0.0, 0.8),
     'L0_ffn_b2': (0.0, 0.8)}
    factors = {'L0_ffn_gate_w': 8.0, 'L0_ffn_W1': 8.0, 'L0_ffn_W2': 8.0}
    for name, (base, spread) in spreads.items():
        noise = np.random.default_rng([zlib.crc32(name.encode()), seed]).standard_normal(out[name].shape)
        drawn = base * np.exp(spread * noise) if base else spread * noise
        out[name] = jnp.asarray(drawn.astype(out[name].dtype))
    for name, factor in factors.items():
        out[name] = (out[name] * factor).astype(out[name].dtype)
    return out
```

```python
from contextlib import ExitStack

import concourse.bass as bass
from concourse import mybir

F32 = mybir.dt.float32
F32R = mybir.dt.float32r
U32 = mybir.dt.uint32
ALU = mybir.AluOpType
ACT = mybir.ActivationFunctionType
AX = mybir.AxisListType


def metaformer_kernel(nc, x, w_reduce, gamma, beta, mean, var, w_span, b_span,
                      gate_w, gate_b, W1, b1, W2, b2, out):
    B, H, W, C = x.shape
    CR = w_reduce.shape[1]
    E = gate_w.shape[1]
    HID = W1.shape[2]
    K = 7
    PAD = K // 2
    G = w_span.shape[1] // (K * K)
    CG = C // G
    assert B == 4 and C == 128 and CR == 32 and HID == 2 * 128
    T = 2 * W
    R = 4
    N = R * T
    QN = H // R
    STEPS = 2 * R
    assert STEPS == E
    WP = W + 2 * PAD
    HP = H + 2 * PAD
    JS = [(0, 4), (4, 3)]
    FOLDS = [2, 2]
    ROWC = K * C
    KR = 3 * CR + 2
    LN1_EPS, LN2_EPS, BN_EPS = 1e-6, 1e-5, 1e-3

    def group(q, bo, d):
        return q + (bo + d) // 2, (bo + d) % 2

    def exists(q):
        return not isinstance(q, int) or 0 <= q < QN

    def some(value):
        return not isinstance(value, int) or value > 0

    ctx = ExitStack()
    with ctx:
        def sb(name, shape, dt=F32):
            return ctx.enter_context(nc.sbuf_tensor(name, shape, dt))

        def bank(name):
            return ctx.enter_context(nc.psum_tensor(name, [128, 512], F32))

        def sem(name):
            return ctx.enter_context(nc.semaphore(name))

        ident = sb("ident", [128, 128])
        minus_half = sb("minus_half", [128, R])
        wred3 = sb("wred3", [128, 3 * CR])
        bn_in = sb("bn_in", [3 * CR, 4])
        bn_ve = sb("bn_ve", [3 * CR, 1])
        bn_rs = sb("bn_rs", [3 * CR, 1])
        bn_scale = sb("bn_scale", [3 * CR, 1])
        bn_ms = sb("bn_ms", [3 * CR, 1])
        bn_bias = sb("bn_bias", [3 * CR, 1])
        wk = sb("wk", [KR, K * K * G], F32R)
        wk_lo = sb("wk_lo", [KR, K * K * G], F32R)
        w1_hi = sb("w1_hi", [128, E * HID], F32R)
        w1_lo = sb("w1_lo", [128, E * HID], F32R)
        b1_t = sb("b1_t", [128, E * 2])
        w2_t = sb("w2_t", [128, E * 2 * C])
        b2_rows = sb("b2_rows", [R * E, R * C])
        gate_raw = sb("gate_raw", [128, E])
        gate_hi = sb("gate_hi", [128, E], F32R)
        gate_lo = sb("gate_lo", [128, E], F32R)
        gate_bias = sb("gate_bias", [128, R * E])
        expert_no = sb("expert_no", [128, R * E])
        x_in = [sb(f"x_in{i}", [128, R * C]) for i in range(2)]
        st1 = sb("st1", [128, R, 6])
        mv1 = [sb(f"{name}1", [128, R, m] if m > 1 else [128, R])
               for name, m in (("both", 3), ("diff", 1), ("var_in", 1), ("sq", 1))]
        ve1 = sb("ve1", [128, R])
        nm1 = sb("nm1", [128, R])
        rs1 = sb("rs1", [128, R])
        nb1 = sb("nb1", [128, R])
        xn = sb("xn", [128, 2 * HP * C])
        stage = [sb(f"stage{i}", [128, R * C]) for i in range(2)]
        xnT = sb("xnT", [128, N])
        r_lin = sb("r_lin", [128, N])
        rT = [sb(f"rT{i}", [KR, R * 2 * WP], F32R) for i in range(2)]
        prod = [sb(f"prod{i}", [128, JS[i % 2][1] * ROWC]) for i in range(4)]
        convT = sb("convT", [128, N])
        x_res = [sb(f"x_res{i}", [128, R * C]) for i in range(2)]
        t_row = sb("t_row", [128, R * C])
        st2 = sb("st2", [128, R, 6])
        mv2 = [sb(f"{name}2", [128, R, m] if m > 1 else [128, R])
               for name, m in (("both", 3), ("diff", 1), ("var_in", 1), ("sq", 1))]
        ve2 = sb("ve2", [128, R])
        nm2 = sb("nm2", [128, R])
        rs2 = sb("rs2", [128, R])
        nb2 = sb("nb2", [128, R])
        tn = sb("tn", [128, R * C])
        tn_hi = [sb(f"tn_hi{i}", [128, N], F32R) for i in range(2)]
        tn_lo = [sb(f"tn_lo{i}", [128, N], F32R) for i in range(2)]
        logits = sb("logits", [128, R * E])
        lmax = sb("lmax", [128, R])
        lshift = sb("lshift", [128, R * E])
        ex = sb("ex", [128, R * E])
        esum = sb("esum", [128, R])
        erec = sb("erec", [128, R])
        top = sb("top", [128, R, 8])
        topi = sb("topi", [128, R, 8], U32)
        eq0 = sb("eq0", [128, R * E])
        eq1 = sb("eq1", [128, R * E])
        eqs = sb("eqs", [128, R * E])
        exk = sb("exk", [128, R * E])
        cw = [sb(f"cw{i}", [128, R * E]) for i in range(2)]
        cwT = sb("cwT", [R * E, T])
        hT = [[sb(f"hT{i}{f}", [128, N]) for f in range(2)] for i in range(2)]
        acc = [sb(f"acc{i}", [128, R * C]) for i in range(2)]

        kg_bank = [bank("kg0"), bank("kg1")]
        conv_bank = bank("conv")
        misc = bank("misc")
        h_bank = [bank("h0"), bank("h1")]
        y_bank = [bank("y0"), bank("y1")]

        consts_in = sem("consts_in")
        wk_row_in = sem("wk_row_in")
        x_in_loaded = [sem(f"x_in_loaded{i}") for i in range(2)]
        stage_loaded = [sem(f"stage_loaded{i}") for i in range(2)]
        x_res_loaded = [sem(f"x_res_loaded{i}") for i in range(2)]
        out_stored = [sem(f"out_stored{i}") for i in range(2)]
        pool_const = sem("pool_const")
        bn_step = sem("bn_step")
        bn_pow = sem("bn_pow")
        bn_ready = sem("bn_ready")
        split_step = sem("split_step")
        wk_lo_ready = sem("wk_lo_ready")
        ln1_step = sem("ln1_step")
        mv1_ready = sem("mv1_ready")
        pow1_done = sem("pow1_done")
        rstd1_ready = sem("rstd1_ready")
        xn_ready = sem("xn_ready")
        xt_done = sem("xt_done")
        xnT_ready = sem("xnT_ready")
        feat_done = sem("feat_done")
        feat_read = sem("feat_read")
        feat_ready = sem("feat_ready")
        kg_ready = sem("kg_ready")
        prod_done = sem("prod_done")
        fold_step = sem("fold_step")
        folds_done = sem("folds_done")
        conv_done = sem("conv_done")
        convT_ready = sem("convT_ready")
        back_done = sem("back_done")
        t_done = sem("t_done")
        ln2_step = sem("ln2_step")
        mv2_ready = sem("mv2_ready")
        pow2_done = sem("pow2_done")
        rstd2_ready = sem("rstd2_ready")
        tn_ready = sem("tn_ready")
        tnT_done = sem("tnT_done")
        tn_hi_ready = sem("tn_hi_ready")
        tn_lo_ready = sem("tn_lo_ready")
        gate_done = sem("gate_done")
        logits_read = sem("logits_read")
        soft_step = sem("soft_step")
        shift_ready = sem("shift_ready")
        ex_ready = sem("ex_ready")
        cw_ready = sem("cw_ready")
        cwT_done = sem("cwT_done")
        cwT_ready = sem("cwT_ready")
        b2_done = sem("b2_done")
        acc_init = sem("acc_init")
        h_ready = sem("h_ready")
        gelu_done = sem("gelu_done")
        y_done = sem("y_done")
        acc_done = sem("acc_done")

        wk_raw = prod[1][0:KR, 0:K * K * G]
        w1_raw = prod[0][:, 0:E * HID]
        N_CONSTS = (3 + 12 + 5) + (2 + R + 2 + 2 + R)

        block = ctx.enter_context(nc.Block())

        def image_rows(dram, row, bo, bi):
            return dram[2 * bo + bi, bass.ds(row, R), :, :].rearrange("h w c -> w h c")

        def half_rows(tile, bi):
            return tile[bi:T:2, :].rearrange("w (h c) -> w h c", c=C)

        def shifted(tile, r, j):
            lo = 2 * (r * WP + 2 * PAD - j)
            return tile[:, lo:lo + T]

        def interior(tile):
            return tile.rearrange("p (r w) -> p r w", w=2 * WP)[:, :, 2 * PAD:2 * PAD + T]

        @block.sync
        def _(sp):
            def at(value):
                return value if isinstance(value, int) else sp.snap(value)

            def load_x(row, bo):
                for bi in range(2):
                    sp.dma_start(half_rows(x_in[bo], bi), image_rows(x, row, bo, bi)).then_inc(x_in_loaded[bo], 16)

            def load_stage(q, bo):
                n = 2 * q + bo
                lo = at((bo * HP + PAD) * C + R * C * q)
                if some(n - 1):
                    sp.wait_ge(xt_done, n - 1)
                sp.dma_start(stage[bo][0:T, :], xn[0:T, bass.ds(lo, R * C)]) \
                    .then_inc(stage_loaded[bo], 16)

            def slot(q, bo):
                ql, bl = group(q, bo, 3)
                qx, bx = group(q, bo, 1)
                if exists(qx):
                    row = at(R * ql)
                    sp.wait_ge(xn_ready, 2 * q + bo + 2)
                if exists(ql):
                    load_x(row, bl)
                if exists(qx):
                    load_stage(qx, bx)
                qp, bp = group(q, bo, -1)
                if exists(qp):
                    n = 2 * qp + bp
                    row = at(R * qp)
                    if some(n - 1):
                        sp.wait_ge(t_done, n - 1)
                    for bi in range(2):
                        sp.dma_start(half_rows(x_res[bp], bi), image_rows(x, row, bp, bi)) \
                            .then_inc(x_res_loaded[bp], 16)
                qo, bo_ = group(q, bo, -3)
                if exists(qo):
                    store(qo, bo_)

            def store(q, bo):
                row = at(R * q)
                sp.wait_ge(acc_done, E * (2 * q + bo + 1))
                for bi in (1, 0):
                    sp.dma_start(image_rows(out, row, bo, bi), half_rows(acc[bo], bi)).then_inc(out_stored[bo], 16)

            load_x(0, 0)
            load_x(0, 1)
            for c in range(3):
                sp.dma_start(wred3[:, c * CR:(c + 1) * CR], w_reduce).then_inc(consts_in, 16)
                for v, a in enumerate((gamma, beta, mean, var)):
                    sp.dma_start(bn_in[c * CR:(c + 1) * CR, v:v + 1], a.rearrange("(p a) -> p a", a=1)) \
                        .then_inc(consts_in, 16)
            for c in range(3):
                sp.dma_start(wk_raw[c * CR:(c + 1) * CR, :], w_span).then_inc(consts_in, 16)
            for c in range(2):
                sp.dma_start(wk_raw[3 * CR + c:3 * CR + c + 1, :], b_span.rearrange("(a n) -> a n", a=1)) \
                    .then_inc(consts_in, 16)
            sp.wait_ge(xn_ready, 1)
            load_x(R, 0)
            load_stage(0, 0)
            sp.wait_ge(wk_lo_ready, 1)
            sp.dma_start(wk[KR - 1:KR, :].bitcast(F32), wk_lo[KR - 1:KR, :].bitcast(F32)).then_inc(wk_row_in, 16)

            for q in range(2):
                slot(q, 0)
                slot(q, 1)
            with sp.Fori(2, QN - 2) as q:
                slot(q, 0)
                slot(q, 1)
            for q in range(QN - 2, QN + 1):
                slot(q, 0)
                slot(q, 1)
            store(QN - 1, 1)
            for bo in range(2):
                sp.wait_ge(out_stored[bo], 32 * QN)

        @block.gpsimd
        def _(pool):
            pool.memset(ident[:, :], 0.0).then_inc(pool_const, 1)
            pool.memset(minus_half[:, :], -0.5).then_inc(pool_const, 1)
            for i in range(2):
                pool.memset(rT[i][:, :].bitcast(F32), 0.0).then_inc(pool_const, 1)
            pool.memset(b2_rows[:, :], 0.0).then_inc(pool_const, 1)
            for bo in range(2):
                for top_row in (0, PAD + H):
                    lo = (bo * HP + top_row) * C
                    pool.memset(xn[0:T, lo:lo + PAD * C], 0.0).then_inc(pool_const, 1)
            pool.wait_ge(pool_const, 9)
            pool.affine_select(out=ident[:, :], in_=ident[:, :], compare_op=ALU.not_equal, fill=1.0, base=0,
                               pattern=[[-1, 128]], channel_multiplier=1).then_inc(pool_const, 1)
            pool.wait_ge(pool_const, 10)
            for i in range(2):
                pool.memset(rT[i][3 * CR:KR, :].bitcast(F32), 1.0).then_inc(pool_const, 1)
            pool.wait_ge(pool_const, 12)
            for e in range(E):
                pool.memset(expert_no[:, e:R * E:E], float(e)).then_inc(pool_const, 1)
            pool.wait_ge(bn_step, 1)
            nc.gpsimd.tensor_tensor(bn_rs[:, :], bn_ve[:, :], minus_half[0:3 * CR, 0:1], ALU.pow).then_inc(bn_pow, 1)

            def rstd(n, ve, nm, rs, nb, mv_ready, pow_done, ready, used):
                pool.wait_ge(mv_ready, 2 * n + 2)
                if some(n):
                    pool.wait_ge(used, n)
                nc.gpsimd.tensor_tensor(rs[0:T, :], ve[0:T, :], minus_half[0:T, :], ALU.pow).then_inc(pow_done, 1)
                pool.wait_ge(pow_done, n + 1)
                nc.gpsimd.tensor_tensor(nb[0:T, :], nm[0:T, :], rs[0:T, :], ALU.mult).then_inc(ready, 1)

            def rstd1(q, bo):
                rstd(2 * q + bo, ve1, nm1, rs1, nb1, mv1_ready, pow1_done, rstd1_ready, xn_ready)

            def feat_lo(q, bo):
                n = 2 * q + bo
                pool.wait_ge(feat_read, 2 * n + 2)
                inside = interior(rT[bo][2 * CR:3 * CR, :])
                nc.gpsimd.tensor_tensor(inside, r_lin[2 * CR:3 * CR, :].rearrange("p (r w) -> p r w", w=T),
                                        inside.bitcast(F32), ALU.subtract).then_inc(feat_ready, 1)
                pool.wait_ge(feat_ready, n + 1)

            def folds(q, bo, u):
                m = STEPS * (2 * q + bo) + u
                rows = prod[u % 4][0:T, :].rearrange("p (j i) -> p j i", i=ROWC)
                pool.wait_ge(prod_done, m + 1)
                nc.gpsimd.tensor_tensor(rows[:, :, 0:3 * C], rows[:, :, 0:3 * C], rows[:, :, 3 * C:6 * C],
                                        ALU.add).then_inc(fold_step if FOLDS[u % 2] > 1 else folds_done, 1)
                if FOLDS[u % 2] > 1:
                    fm = m + 1 if FOLDS == [2, 2] else STEPS // 2 * (2 * q + bo) + u // 2 + 1
                    pool.wait_ge(fold_step, fm)
                    nc.gpsimd.tensor_tensor(rows[:, :, 0:C], rows[:, :, 0:C], rows[:, :, 6 * C:7 * C],
                                            ALU.add).then_inc(folds_done, 1)

            def slot(q, bo):
                for u in range(STEPS):
                    if exists(q):
                        folds(q, bo, u)
                    qp, bp = group(q, bo, -1)
                    if u == 2 and exists(qp):
                        rstd(2 * qp + bp, ve2, nm2, rs2, nb2, mv2_ready, pow2_done, rstd2_ready, tn_ready)
                    ql, bl = group(q, bo, 3)
                    if u == 3 and exists(ql):
                        rstd1(ql, bl)
                    qx, bx = group(q, bo, 1)
                    if u == 4 and exists(qx):
                        pool.wait_ge(folds_done, STEPS * (2 * q + bo) + u + 1)
                        feat_lo(qx, bx)

            for d in range(3):
                rstd1(*group(0, 0, d))
                if d == 0:
                    pool.wait_ge(rstd1_ready, 1)
                    feat_lo(0, 0)
            for q in range(2):
                slot(q, 0)
                slot(q, 1)
            with pool.Fori(2, QN - 2) as q:
                slot(q, 0)
                slot(q, 1)
            for q in range(QN - 2, QN + 1):
                slot(q, 0)
                slot(q, 1)

        @block.scalar
        def _(act):
            act.dma_start(w1_raw.rearrange("p (e h) -> p e h", e=E), W1.rearrange("e d h -> d e h")) \
                .then_inc(consts_in, 16)
            act.dma_start(gate_raw[:, :], gate_w).then_inc(consts_in, 16)
            for r in range(R):
                act.dma_start(gate_bias[0:T, r * E:(r + 1) * E], gate_b.partition_broadcast(T)) \
                    .then_inc(consts_in, 16)
            with nc.allow_non_contiguous_dma(reason="2048 bias values, once"):
                for f in range(2):
                    act.dma_start(b1_t[:, f:2 * E:2], b1[:, f * 128:(f + 1) * 128].rearrange("e p -> p e")) \
                        .then_inc(consts_in, 16)

            for f in range(2):
                act.dma_start(w2_t[:, :].rearrange("p (e f c) -> p e f c", e=E, f=2)[:, :, f, :],
                              W2[:, f * 128:(f + 1) * 128, :].rearrange("e p c -> p e c")).then_inc(consts_in, 16)
            act.wait_ge(pool_const, 9)
            for r in range(R):
                act.dma_start(b2_rows[r * E:(r + 1) * E, r * C:(r + 1) * C], b2).then_inc(consts_in, 16)

            def apply1(q, bo):
                n = 2 * q + bo
                act.wait_ge(rstd1_ready, n + 1)
                for r in range(R):
                    ins = act.activation(xn[0:T, bass.ds((bo * HP + PAD + r) * C + R * C * q, C)],
                                         x_in[bo][0:T, r * C:(r + 1) * C], ACT.Identity,
                                         bias=nb1[0:T, r:r + 1], scale=rs1[0:T, r:r + 1])
                ins.then_inc(xn_ready, 1)

            def take_xnT(q, bo):
                n = 2 * q + bo
                act.wait_ge(xt_done, n + 1)
                if some(n):
                    act.wait_ge(feat_done, n)
                act.activation(xnT[:, :], misc[:, 0:N], ACT.Copy).then_inc(xnT_ready, 1)

            def features(q, bo):
                n = 2 * q + bo
                act.wait_ge(feat_done, n + 1)
                if some(n - 1):
                    act.wait_ge(kg_ready, STEPS * (n - 1))
                if some(n):
                    act.wait_ge(feat_ready, n)
                act.activation(interior(rT[bo][0:3 * CR, :]),
                               misc[0:3 * CR, 0:N].rearrange("p (r w) -> p r w", w=T),
                               ACT.Relu, bias=bn_bias[:, :], scale=bn_scale[:, :]).then_inc(feat_read, 1)
                act.activation(r_lin[2 * CR:3 * CR, :], misc[2 * CR:3 * CR, 0:N], ACT.Relu,
                               bias=bn_bias[2 * CR:3 * CR, :], scale=bn_scale[2 * CR:3 * CR, :]) \
                    .then_inc(feat_read, 1)

            def take_conv(q, bo):
                n = 2 * q + bo
                act.wait_ge(conv_done, STEPS * (n + 1))
                if some(n):
                    act.wait_ge(back_done, n)
                act.activation(convT[:, :].rearrange("p (r w) -> p r w", w=T),
                               interior(conv_bank[:, 0:R * 2 * WP]), ACT.Copy).then_inc(convT_ready, 1)

            def apply2(q, bo):
                n = 2 * q + bo
                act.wait_ge(rstd2_ready, n + 1)
                if some(n):
                    act.wait_ge(tnT_done, n)
                for r in range(R):
                    ins = act.activation(tn[0:T, r * C:(r + 1) * C], t_row[0:T, r * C:(r + 1) * C], ACT.Identity,
                                         bias=nb2[0:T, r:r + 1], scale=rs2[0:T, r:r + 1])
                ins.then_inc(tn_ready, 1)

            def take_tn_hi(q, bo):
                n = 2 * q + bo
                act.wait_ge(tnT_done, n + 1)
                if some(n - 1):
                    act.wait_ge(h_ready, 2 * E * (n - 1))
                act.activation(tn_hi[bo][:, :], misc[:, 0:N], ACT.Copy).then_inc(tn_hi_ready, 1)

            def exps(q, bo):
                n = 2 * q + bo
                act.wait_ge(shift_ready, n + 1)
                if some(n):
                    act.wait_ge(cw_ready, n)
                act.activation(ex[0:T, :], lshift[0:T, :], ACT.Exp).then_inc(ex_ready, 1)

            def gelus(q, bo, e):
                m = E * (2 * q + bo) + e
                for f in range(2):
                    act.wait_ge(h_ready, 2 * m + f + 1)
                    if some(m - 1):
                        act.wait_ge(y_done, m - 1)
                    act.activation(hT[e % 2][f][:, :], h_bank[f][:, 0:N], ACT.Gelu,
                                   bias=b1_t[:, 2 * e + f:2 * e + f + 1]).then_inc(gelu_done, 1)

            def slot(q, bo):
                for u in range(STEPS):
                    qe, be = group(q, bo, -2)
                    if exists(qe):
                        gelus(qe, be, u)
                    ql, bl = group(q, bo, 3)
                    qx, bx = group(q, bo, 1)
                    qp, bp = group(q, bo, -1)
                    if u == 1 and exists(qx):
                        take_xnT(qx, bx)
                    if u == 1 and exists(qp):
                        take_conv(qp, bp)
                    if u == 3 and exists(qx):
                        features(qx, bx)
                    if u == 3 and exists(qp):
                        apply2(qp, bp)
                    if u == 4 and exists(qp):
                        take_tn_hi(qp, bp)
                    if u == 4 and exists(ql):
                        apply1(ql, bl)
                    if u == 6 and exists(qp):
                        exps(qp, bp)

            for d in range(3):
                apply1(*group(0, 0, d))
                if d == 0:
                    take_xnT(0, 0)
                    act.wait_ge(bn_ready, 2)
                    act.wait_ge(pool_const, 20)
                    features(0, 0)
            act.wait_ge(consts_in, 16 * N_CONSTS)
            for q in range(2):
                slot(q, 0)
                slot(q, 1)
            with act.Fori(2, QN - 2) as q:
                slot(q, 0)
                slot(q, 1)
            for q in range(QN - 2, QN + 1):
                slot(q, 0)
                slot(q, 1)

        @block.vector
        def _(dve):
            def moments(n, src, st, both, diff, var_in, sq, ve, nm, eps, step, ready, used):
                for r in range(R):
                    ins = dve.bn_stats(st[0:T, r, :], src[0:T, r * C:(r + 1) * C])
                ins.then_inc(step, 1)
                dve.wait_ge(step, 3 * n + 1)
                nc.vector.tensor_tensor(both[0:T], st[0:T, :, 0:3], st[0:T, :, 3:6], ALU.add)
                nc.vector.tensor_tensor(diff[0:T, :], st[0:T, :, 1], st[0:T, :, 4], ALU.subtract).then_inc(step, 1)
                dve.wait_ge(step, 3 * n + 2)
                if some(n):
                    dve.wait_ge(used, n)
                dve.tensor_scalar(nm[0:T, :], both[0:T, :, 1], -0.5, None, ALU.mult).then_inc(ready, 1)
                dve.tensor_scalar(var_in[0:T, :], both[0:T, :, 2], 1.0 / C, eps, ALU.mult, ALU.add)
                dve.scalar_tensor_tensor(out=sq[0:T, :], in0=diff[0:T, :], scalar=0.25, in1=diff[0:T, :],
                                         op0=ALU.mult, op1=ALU.mult).then_inc(step, 1)
                dve.wait_ge(step, 3 * n + 3)
                nc.vector.tensor_tensor(ve[0:T, :], var_in[0:T, :], sq[0:T, :], ALU.add).then_inc(ready, 1)

            def moments1(q, bo):
                dve.wait_ge(x_in_loaded[bo], 32 * q + 32)
                moments(2 * q + bo, x_in[bo], st1, *mv1, ve1, nm1, LN1_EPS, ln1_step, mv1_ready, rstd1_ready)

            def products(q, bo, u):
                m = STEPS * (2 * q + bo) + u
                r, half = u // 2, u % 2
                jn = JS[half][1]
                if u == 0:
                    qn, _ = group(q, bo, 2)
                    dve.wait_ge(xn_ready, 2 * q + bo + 3 if exists(qn) else 2 * QN)
                dve.wait_ge(kg_ready, m + 1)
                if some(m - 3):
                    dve.wait_ge(conv_done, m - 3)
                xs = xn[0:T, bass.ds((bo * HP + r) * C + R * C * q, ROWC)]
                xs = xs.rearrange("p (a b) -> p a b", b=CG).unsqueeze(1).to_broadcast([T, jn, K * G, CG])
                ks = kg_bank[half][0:T, 0:jn * K * G].rearrange("p (j a) -> p j a", j=jn)
                ks = ks.unsqueeze(3).to_broadcast([T, jn, K * G, CG])
                po = prod[u % 4][0:T, :].rearrange("p (j a b) -> p j a b", j=jn, b=CG)
                nc.vector.tensor_tensor(po, ks, xs, ALU.mult).then_inc(prod_done, 1)

            def add_expert(q, bo, e):
                m = E * (2 * q + bo) + e
                dve.wait_ge(y_done, m + 1)
                if e == 0:
                    dve.wait_ge(acc_init, 2 * q + bo + 1)
                else:
                    dve.wait_ge(acc_done, m)
                for r in range(R):
                    rows = acc[bo][0:T, r * C:(r + 1) * C]
                    ins = dve.scalar_tensor_tensor(out=rows, in0=y_bank[e % 2][0:T, r * C:(r + 1) * C],
                                                   scalar=cw[bo][0:T, r * E + e:r * E + e + 1], in1=rows,
                                                   op0=ALU.mult, op1=ALU.add)
                ins.then_inc(acc_done, 1)

            def start_acc(q, bo):
                n = 2 * q + bo
                dve.wait_ge(b2_done, n + 1)
                dve.wait_ge(t_done, n + 1)
                if some(q):
                    dve.wait_ge(out_stored[bo], 32 * q)
                nc.vector.tensor_tensor(acc[bo][0:T, :], misc[0:T, 0:R * C], t_row[0:T, :], ALU.add) \
                    .then_inc(acc_init, 1)

            def residual(q, bo):
                n = 2 * q + bo
                dve.wait_ge(back_done, n + 1)
                dve.wait_ge(x_res_loaded[bo], 32 * q + 32)
                if some(n):
                    dve.wait_ge(acc_init, n)
                    dve.wait_ge(tn_ready, n)
                nc.vector.tensor_tensor(t_row[0:T, :], misc[0:T, 0:R * C], x_res[bo][0:T, :], ALU.add) \
                    .then_inc(t_done, 1)
                dve.wait_ge(t_done, n + 1)
                moments(n, t_row, st2, *mv2, ve2, nm2, LN2_EPS, ln2_step, mv2_ready, rstd2_ready)

            def take_tn_lo(q, bo):
                dve.wait_ge(tn_hi_ready, 2 * q + bo + 1)
                nc.vector.tensor_tensor(tn_lo[bo][:, :], misc[:, 0:N], tn_hi[bo][:, :].bitcast(F32), ALU.subtract) \
                    .then_inc(tn_lo_ready, 1)

            def per_row(tile):
                return tile[0:T, :].rearrange("p (r e) -> p r e", e=E)

            def spread(tile):
                return tile.to_broadcast([T, R, E])

            SOFT = 9

            def shift_logits(q, bo):
                n = 2 * q + bo
                dve.wait_ge(gate_done, n + 1)
                nc.vector.tensor_tensor(logits[0:T, :], misc[0:T, 0:R * E], gate_bias[0:T, :], ALU.add) \
                    .then_inc(logits_read, 1)
                dve.wait_ge(logits_read, n + 1)
                dve.tensor_reduce(lmax[0:T, :], per_row(logits), AX.X, ALU.max).then_inc(soft_step, 1)
                dve.wait_ge(soft_step, SOFT * n + 1)
                if some(n):
                    dve.wait_ge(ex_ready, n)
                nc.vector.tensor_tensor(per_row(lshift), per_row(logits), spread(lmax[0:T, :].unsqueeze(2)),
                                        ALU.subtract).then_inc(shift_ready, 1)

            def top2_weights(q, bo):
                n = 2 * q + bo
                dve.wait_ge(ex_ready, n + 1)
                dve.tensor_reduce(esum[0:T, :], per_row(ex), AX.X, ALU.add).then_inc(soft_step, 1)
                for r in range(R):
                    ins = dve.max(top[0:T, r, :], ex[0:T, r * E:(r + 1) * E])
                ins.then_inc(soft_step, 1)
                dve.wait_ge(soft_step, SOFT * n + 3)
                dve.reciprocal(erec[0:T, :], esum[0:T, :]).then_inc(soft_step, 1)
                for r in range(R):
                    ins = dve.max_index(topi[0:T, r, :], top[0:T, r, :], ex[0:T, r * E:(r + 1) * E])
                ins.then_inc(soft_step, 1)
                dve.wait_ge(soft_step, SOFT * n + 5)
                for c, eq in enumerate((eq0, eq1)):
                    nc.vector.tensor_tensor(per_row(eq), per_row(expert_no), spread(topi[0:T, :, c:c + 1]),
                                            ALU.is_equal).then_inc(soft_step, 1)
                dve.wait_ge(soft_step, SOFT * n + 7)
                nc.vector.tensor_tensor(eqs[0:T, :], eq0[0:T, :], eq1[0:T, :], ALU.add).then_inc(soft_step, 1)
                nc.vector.tensor_tensor(per_row(exk), per_row(ex), spread(erec[0:T, :].unsqueeze(2)),
                                        ALU.mult).then_inc(soft_step, 1)
                dve.wait_ge(soft_step, SOFT * n + 9)
                nc.vector.tensor_tensor(cw[bo][0:T, :], exk[0:T, :], eqs[0:T, :], ALU.mult).then_inc(cw_ready, 1)

            def take_cwT(q, bo):
                n = 2 * q + bo
                dve.wait_ge(cwT_done, n + 1)
                if some(n):
                    dve.wait_ge(b2_done, n)
                dve.tensor_copy(cwT[:, :], misc[0:R * E, 0:T]).then_inc(cwT_ready, 1)

            def slot(q, bo):
                for u in range(STEPS):
                    if exists(q):
                        products(q, bo, u)
                    qe, be = group(q, bo, -3 if u == 0 else -2)
                    if exists(qe):
                        add_expert(qe, be, (u - 1) % E)
                    qg, bg = group(q, bo, -2)
                    if u == 0 and exists(qg):
                        start_acc(qg, bg)
                    qp, bp = group(q, bo, -1)
                    ql, bl = group(q, bo, 3)
                    if u == 3 and exists(ql):
                        moments1(ql, bl)
                    if not exists(qp):
                        continue
                    if u == 2:
                        residual(qp, bp)
                    if u == 4:
                        take_tn_lo(qp, bp)
                    if u == 5:
                        shift_logits(qp, bp)
                    if u == 6:
                        top2_weights(qp, bp)
                    if u == 7:
                        take_cwT(qp, bp)

            moments1(0, 0)
            dve.wait_ge(consts_in, 16 * N_CONSTS)
            dve.tensor_scalar(bn_ve[:, :], bn_in[:, 3:4], BN_EPS, None, ALU.add).then_inc(bn_step, 1)
            wk_order = wk_raw.rearrange("p (g i j) -> p j i g", g=G, i=K)
            for j in range(K):
                dve.tensor_copy(wk[:, j * K * G:(j + 1) * K * G].rearrange("p (i g) -> p i g", g=G),
                                wk_order[:, j, :, :]).then_inc(split_step, 1)
            dve.wait_ge(split_step, K)
            for j in range(K):
                part = slice(j * K * G, (j + 1) * K * G)
                ins = nc.vector.tensor_tensor(wk_lo[:, part].rearrange("p (i g) -> p i g", g=G), wk_order[:, j, :, :],
                                              wk[:, part].bitcast(F32).rearrange("p (i g) -> p i g", g=G),
                                              ALU.subtract)
            ins.then_inc(wk_lo_ready, 1)
            dve.wait_ge(wk_lo_ready, 1)
            dve.tensor_copy(wk[CR:2 * CR, :], wk_lo[CR:2 * CR, :].bitcast(F32)).then_inc(split_step, 1)
            dve.wait_ge(bn_pow, 1)
            nc.vector.tensor_tensor(bn_scale[:, :], bn_rs[:, :], bn_in[:, 0:1], ALU.mult).then_inc(bn_ready, 1)
            dve.wait_ge(bn_ready, 1)
            nc.vector.tensor_tensor(bn_ms[:, :], bn_scale[:, :], bn_in[:, 2:3], ALU.mult).then_inc(bn_step, 1)
            dve.wait_ge(bn_step, 2)
            nc.vector.tensor_tensor(bn_bias[:, :], bn_in[:, 1:2], bn_ms[:, :], ALU.subtract).then_inc(bn_ready, 1)
            moments1(0, 1)
            dve.tensor_copy(w1_hi[:, :], w1_raw).then_inc(split_step, 1)
            dve.tensor_copy(gate_hi[:, :], gate_raw[:, :]).then_inc(split_step, 1)
            dve.wait_ge(split_step, K + 3)
            nc.vector.tensor_tensor(w1_lo[:, :], w1_raw, w1_hi[:, :].bitcast(F32), ALU.subtract).then_inc(split_step, 1)
            nc.vector.tensor_tensor(gate_lo[:, :], gate_raw[:, :], gate_hi[:, :].bitcast(F32), ALU.subtract) \
                .then_inc(split_step, 1)
            moments1(1, 0)
            dve.wait_ge(split_step, K + 5)
            dve.wait_ge(pool_const, 20)
            for q in range(2):
                slot(q, 0)
                slot(q, 1)
            with dve.Fori(2, QN - 2) as q:
                slot(q, 0)
                slot(q, 1)
            for q in range(QN - 2, QN + 1):
                slot(q, 0)
                slot(q, 1)
            add_expert(QN - 1, 1, E - 1)

        @block.tensor
        def _(pe):
            ident_row = ident[0:T, 0:T]

            def transpose_in(q, bo):
                n = 2 * q + bo
                pe.wait_ge(stage_loaded[bo], 16 * q + 16)
                if some(n):
                    pe.wait_ge(feat_read, 2 * n)
                if some(n - 2):
                    pe.wait_ge(acc_init, n - 2)
                for r in range(R):
                    mm = pe.transpose(misc[:, r * T:(r + 1) * T], stage[bo][0:T, r * C:(r + 1) * C], ident_row)
                mm.then_inc(xt_done, 1)

            def reduce_channels(q, bo):
                n = 2 * q + bo
                pe.wait_ge(xnT_ready, n + 1)
                if some(n - 1):
                    pe.wait_ge(t_done, n - 1)
                pe.matmul(misc[0:3 * CR, 0:N], wred3[:, :], xnT[:, :], start=True, stop=True) \
                    .then_inc(feat_done, 1)

            def kernels(q, bo, u):
                m = STEPS * (2 * q + bo) + u
                r, half = u // 2, u % 2
                if u == 0:
                    pe.wait_ge(feat_ready, 2 * q + bo + 1)
                if some(m - 1):
                    pe.wait_ge(prod_done, m - 1)
                j0, jn = JS[half]
                for j in range(j0, j0 + jn):
                    mm = pe.matmul(kg_bank[half][0:T, (j - j0) * K * G:(j - j0 + 1) * K * G],
                                   shifted(rT[bo], r, j), wk[:, j * K * G:(j + 1) * K * G],
                                   start=True, stop=True)
                mm.then_inc(kg_ready, 1)

            def gather_taps(q, bo, u):
                m = STEPS * (2 * q + bo) + u
                r, half = u // 2, u % 2
                pe.wait_ge(folds_done, m + 1)
                if u == 0 and some(2 * q + bo):
                    pe.wait_ge(convT_ready, 2 * q + bo)
                j0, jn = JS[half]
                kept = [0, 1, 2] if FOLDS[half] > 1 else [0, 1, 2, 6]
                for j in range(j0, j0 + jn):
                    for i in kept:
                        at = (j - j0) * ROWC + i * C
                        mm = pe.matmul(shifted(conv_bank, r, j), prod[u % 4][0:T, at:at + C],
                                       ident_row, is_transpose=True,
                                       start=(u == 0 and j == j0 and i == 0),
                                       stop=(u == STEPS - 1 and j == K - 1 and i == kept[-1]),
                                       skip_group_check=True)
                mm.then_inc(conv_done, 1)

            def transpose_back(q, bo):
                n = 2 * q + bo
                qx, _ = group(q, bo, 2)
                pe.wait_ge(convT_ready, n + 1)
                if exists(qx):
                    pe.wait_ge(xnT_ready, n + 3)
                else:
                    pe.wait_ge(acc_init, n)
                for r in range(R):
                    mm = pe.transpose(misc[0:T, r * C:(r + 1) * C], convT[:, r * T:(r + 1) * T], ident[:, :])
                mm.then_inc(back_done, 1)

            def transpose_tn(q, bo):
                n = 2 * q + bo
                qx, _ = group(q, bo, 2)
                pe.wait_ge(tn_ready, n + 1)
                if exists(qx):
                    pe.wait_ge(feat_read, 2 * n + 6)
                for r in range(R):
                    mm = pe.transpose(misc[:, r * T:(r + 1) * T], tn[0:T, r * C:(r + 1) * C], ident_row)
                mm.then_inc(tnT_done, 1)

            def gate(q, bo):
                pe.wait_ge(tn_lo_ready, 2 * q + bo + 1)
                for r in range(R):
                    at = slice(r * T, (r + 1) * T)
                    to = misc[0:T, r * E:(r + 1) * E]
                    pe.matmul(to, tn_hi[bo][:, at], gate_hi[:, :], start=True, stop=False)
                    pe.matmul(to, tn_hi[bo][:, at], gate_lo[:, :], start=False, stop=False)
                    mm = pe.matmul(to, tn_lo[bo][:, at], gate_hi[:, :], start=False, stop=True)
                mm.then_inc(gate_done, 1)

            def transpose_cw(q, bo):
                n = 2 * q + bo
                pe.wait_ge(cw_ready, n + 1)
                pe.wait_ge(logits_read, n + 1)
                pe.transpose(misc[0:R * E, 0:T], cw[bo][0:T, :], ident_row).then_inc(cwT_done, 1)

            def expert_bias(q, bo):
                pe.wait_ge(cwT_ready, 2 * q + bo + 1)
                for r in range(R):
                    mm = pe.matmul(misc[0:T, r * C:(r + 1) * C], cwT[:, :], b2_rows[:, r * C:(r + 1) * C],
                                   start=True, stop=True)
                mm.then_inc(b2_done, 1)

            def expert_in(q, bo, e):
                m = E * (2 * q + bo) + e
                if e == 0:
                    pe.wait_ge(tn_lo_ready, 2 * q + bo + 1)
                for f in range(2):
                    if some(m):
                        pe.wait_ge(gelu_done, 2 * m - 1 + f)
                    at = slice(e * HID + f * 128, e * HID + (f + 1) * 128)
                    to = h_bank[f][:, 0:N]
                    pe.matmul(to, w1_hi[:, at], tn_hi[bo][:, :], start=True, stop=False)
                    pe.matmul(to, w1_hi[:, at], tn_lo[bo][:, :], start=False, stop=False)
                    pe.matmul(to, w1_lo[:, at], tn_hi[bo][:, :], start=False, stop=True).then_inc(h_ready, 1)

            def expert_out(q, bo, e):
                m = E * (2 * q + bo) + e
                pe.wait_ge(gelu_done, 2 * m + 2)
                if some(m - 1):
                    pe.wait_ge(acc_done, m - 1)
                for r in range(R):
                    for f in range(2):
                        mm = pe.matmul(y_bank[e % 2][0:T, r * C:(r + 1) * C], hT[e % 2][f][:, r * T:(r + 1) * T],
                                       w2_t[:, (2 * e + f) * C:(2 * e + f + 1) * C], start=(f == 0), stop=(f == 1))
                mm.then_inc(y_done, 1)

            def slot(q, bo):
                qx, bx = group(q, bo, 1)
                qp, bp = group(q, bo, -1)
                qe, be = group(q, bo, -2)
                for u in range(STEPS):
                    qk, bk = (q, bo) if u < STEPS - 1 else (qx, bx)
                    if exists(qk):
                        kernels(qk, bk, (u + 1) % STEPS)
                    if exists(qe):
                        expert_in(qe, be, u)
                    if u == 0 and exists(qe):
                        expert_bias(qe, be)
                    if u == 1 and exists(qx):
                        transpose_in(qx, bx)
                    if u == 2 and exists(qp):
                        transpose_back(qp, bp)
                    if u == 3 and exists(qx):
                        reduce_channels(qx, bx)
                    if u == 4 and exists(qp):
                        transpose_tn(qp, bp)
                    if u == 5 and exists(qp):
                        gate(qp, bp)
                    if u == 7 and exists(qp):
                        transpose_cw(qp, bp)
                    qc, bc = (qp, bp) if u < 2 else (q, bo)
                    if exists(qc):
                        gather_taps(qc, bc, (u - 2) % STEPS)
                    if exists(qe):
                        expert_out(qe, be, u)

            pe.wait_ge(pool_const, 20)
            pe.wait_ge(consts_in, 16 * N_CONSTS)
            transpose_in(0, 0)
            reduce_channels(0, 0)
            pe.wait_ge(split_step, K + 5)
            pe.wait_ge(wk_row_in, 16)
            kernels(0, 0, 0)
            for q in range(2):
                slot(q, 0)
                slot(q, 1)
            with pe.Fori(2, QN - 2) as q:
                slot(q, 0)
                slot(q, 1)
            for q in range(QN - 2, QN + 1):
                slot(q, 0)
                slot(q, 1)


_INS = ['x', 'L0_conv_w_reduce', 'L0_conv_gamma', 'L0_conv_beta', 'L0_conv_mean', 'L0_conv_var', 'L0_conv_w_span',
        'L0_conv_b_span', 'L0_ffn_gate_w', 'L0_ffn_gate_b', 'L0_ffn_W1', 'L0_ffn_b1', 'L0_ffn_W2', 'L0_ffn_b2']
_OUTS = [((4, 56, 56, 128), 'float32')]


def kernel(**inputs):
    import numpy as _np
    import concourse.bacc as _bacc
    from concourse import mybir as _mybir
    from concourse.bass_utils import run_bass_kernel_spmd as _run

    nc = _bacc.Bacc("TRN2", target_bir_lowering=False, num_devices=1)
    arrays, args = {}, []
    for name in _INS:
        a = _np.ascontiguousarray(inputs[name])
        arrays[f"in_{name}_dram"] = a
        args.append(nc.dram_tensor(f"in_{name}_dram", a.shape, _mybir.dt.from_np(a.dtype), kind="ExternalInput").ap())
    for i, (shape, dtype) in enumerate(_OUTS):
        dt = _mybir.dt.from_np(_np.dtype(dtype))
        args.append(nc.dram_tensor(f"out_{i}_dram", shape, dt, kind="ExternalOutput").ap())
    metaformer_kernel(nc, *args)
    r = _run(nc, [arrays], core_ids=[0])
    got = tuple(r.results[0][f"out_{i}_dram"] for i in range(len(_OUTS)))
    return got[0]
```

```python
from contextlib import ExitStack

import concourse.bass as bass
from concourse import mybir

F32 = mybir.dt.float32
F32R = mybir.dt.float32r
U32 = mybir.dt.uint32
ALU = mybir.AluOpType
ACT = mybir.ActivationFunctionType
AX = mybir.AxisListType


def metaformer_kernel(nc, x, w_reduce, gamma, beta, mean, var, w_span, b_span,
                      gate_w, gate_b, W1, b1, W2, b2, out):
    B, H, W, C = x.shape
    CR = w_reduce.shape[1]
    E = gate_w.shape[1]
    HID = W1.shape[2]
    K = 7
    PAD = K // 2
    G = w_span.shape[1] // (K * K)
    CG = C // G
    assert B == 4 and C == 128 and CR == 32 and HID == 2 * 128
    T = 2 * W
    R = 4
    N = R * T
    QN = H // R
    STEPS = 2 * R
    assert STEPS == E
    WP = W + 2 * PAD
    HP = H + 2 * PAD
    JS = [(0, 4), (4, 3)]
    FOLDS = [2, 2]
    ROWC = K * C
    KR = 3 * CR + 2
    LN1_EPS, LN2_EPS, BN_EPS = 1e-6, 1e-5, 1e-3
    LAG_IN, LAG_OUT, LAG_ADD = 13, 14, 15

    def group(q, bo, d):
        return q + (bo + d) // 2, (bo + d) % 2

    def expert_at(q, bo, u, lag):
        d, e = divmod(u - lag, STEPS)
        return (*group(q, bo, d), e)

    def exists(q):
        return not isinstance(q, int) or 0 <= q < QN

    def some(value):
        return not isinstance(value, int) or value > 0

    ctx = ExitStack()
    with ctx:
        def sb(name, shape, dt=F32):
            return ctx.enter_context(nc.sbuf_tensor(name, shape, dt))

        def bank(name):
            return ctx.enter_context(nc.psum_tensor(name, [128, 512], F32))

        def sem(name):
            return ctx.enter_context(nc.semaphore(name))

        ident = sb("ident", [128, 128])
        minus_half = sb("minus_half", [128, R])
        wred3 = sb("wred3", [128, 3 * CR])
        bn_rows = sb("bn_rows", [4, 3 * CR])
        bn_in = sb("bn_in", [3 * CR, 4])
        bn_ve = sb("bn_ve", [3 * CR, 1])
        bn_rs = sb("bn_rs", [3 * CR, 1])
        bn_scale = sb("bn_scale", [3 * CR, 1])
        bn_ms = sb("bn_ms", [3 * CR, 1])
        bn_bias = sb("bn_bias", [3 * CR, 1])
        wk = sb("wk", [KR, K * K * G], F32R)
        wk_lo = sb("wk_lo", [KR, K * K * G], F32R)
        w1_raw = sb("w1_raw", [128, E * HID])
        w1_hi = sb("w1_hi", [128, E * HID], F32R)
        w1_lo = sb("w1_lo", [128, E * HID], F32R)
        b1_t = sb("b1_t", [128, E * 2])
        w2_t = sb("w2_t", [128, E * 2 * C])
        b2_rows = sb("b2_rows", [R * E, R * C])
        gate_raw = sb("gate_raw", [128, E])
        gate_hi = sb("gate_hi", [128, E], F32R)
        gate_lo = sb("gate_lo", [128, E], F32R)
        gate_bias = sb("gate_bias", [128, R * E])
        expert_no = sb("expert_no", [128, R * E])
        x_in = [sb(f"x_in{i}", [128, R * C]) for i in range(2)]
        st1 = sb("st1", [128, R, 6])
        mv1 = [sb(f"{name}1", [128, R, m] if m > 1 else [128, R])
               for name, m in (("both", 3), ("diff", 1), ("var_in", 1), ("sq", 1))]
        ve1 = sb("ve1", [128, R])
        nm1 = sb("nm1", [128, R])
        rs1 = sb("rs1", [128, R])
        nb1 = sb("nb1", [128, R])
        xn = sb("xn", [128, 2 * HP * C])
        stage = [sb(f"stage{i}", [128, R * C]) for i in range(2)]
        xnT = sb("xnT", [128, N])
        r_lin = sb("r_lin", [128, N])
        rT = [sb(f"rT{i}", [KR, R * 2 * WP], F32R) for i in range(2)]
        prod = [sb(f"prod{i}", [128, JS[i % 2][1] * ROWC]) for i in range(4)]
        convT = sb("convT", [128, N])
        x_res = [sb(f"x_res{i}", [128, R * C]) for i in range(2)]
        t_row = sb("t_row", [128, R * C])
        st2 = sb("st2", [128, R, 6])
        mv2 = [sb(f"{name}2", [128, R, m] if m > 1 else [128, R])
               for name, m in (("both", 3), ("diff", 1), ("var_in", 1), ("sq", 1))]
        ve2 = sb("ve2", [128, R])
        nm2 = sb("nm2", [128, R])
        rs2 = sb("rs2", [128, R])
        nb2 = sb("nb2", [128, R])
        tn = sb("tn", [128, R * C])
        tn_hi = [sb(f"tn_hi{i}", [128, N], F32R) for i in range(2)]
        tn_lo = [sb(f"tn_lo{i}", [128, N], F32R) for i in range(2)]
        logits = sb("logits", [128, R * E])
        lmax = sb("lmax", [128, R])
        lshift = sb("lshift", [128, R * E])
        ex = sb("ex", [128, R * E])
        esum = sb("esum", [128, R])
        erec = sb("erec", [128, R])
        top = sb("top", [128, R, 8])
        topi = sb("topi", [128, R, 8], U32)
        eq0 = sb("eq0", [128, R * E])
        eq1 = sb("eq1", [128, R * E])
        eqs = sb("eqs", [128, R * E])
        exk = sb("exk", [128, R * E])
        cw = [sb(f"cw{i}", [128, R * E]) for i in range(2)]
        cwT = sb("cwT", [R * E, T])
        hT = [[sb(f"hT{i}{f}", [128, N]) for f in range(2)] for i in range(2)]
        acc = [sb(f"acc{i}", [128, R * C]) for i in range(2)]

        kg_bank = [bank("kg0"), bank("kg1")]
        conv_bank = bank("conv")
        misc = bank("misc")
        h_bank = [bank("h0"), bank("h1")]
        y_bank = [bank("y0"), bank("y1")]

        feature_in = sem("feature_in")
        bn_rows_in = sem("bn_rows_in")
        bn_turned = sem("bn_turned")
        expert_in_sb = sem("expert_in_sb")
        wk_row_in = sem("wk_row_in")
        x_in_loaded = [sem(f"x_in_loaded{i}") for i in range(2)]
        stage_loaded = [sem(f"stage_loaded{i}") for i in range(2)]
        x_res_loaded = [sem(f"x_res_loaded{i}") for i in range(2)]
        out_stored = [sem(f"out_stored{i}") for i in range(2)]
        pool_const = sem("pool_const")
        bn_step = sem("bn_step")
        bn_pow = sem("bn_pow")
        bn_ready = sem("bn_ready")
        split_step = sem("split_step")
        wk_lo_ready = sem("wk_lo_ready")
        w1_hi_ready = sem("w1_hi_ready")
        experts_split = sem("experts_split")
        ln1_step = sem("ln1_step")
        mv1_ready = sem("mv1_ready")
        pow1_done = sem("pow1_done")
        rstd1_ready = sem("rstd1_ready")
        xn_ready = sem("xn_ready")
        xt_done = sem("xt_done")
        xnT_ready = sem("xnT_ready")
        feat_done = sem("feat_done")
        feat_read = sem("feat_read")
        feat_ready = sem("feat_ready")
        kg_ready = sem("kg_ready")
        prod_done = sem("prod_done")
        fold_step = sem("fold_step")
        folds_done = sem("folds_done")
        conv_done = sem("conv_done")
        convT_ready = sem("convT_ready")
        back_done = sem("back_done")
        t_done = sem("t_done")
        ln2_step = sem("ln2_step")
        mv2_ready = sem("mv2_ready")
        pow2_done = sem("pow2_done")
        rstd2_ready = sem("rstd2_ready")
        tn_ready = sem("tn_ready")
        tnT_done = sem("tnT_done")
        tn_hi_ready = sem("tn_hi_ready")
        tn_lo_ready = sem("tn_lo_ready")
        gate_done = sem("gate_done")
        logits_read = sem("logits_read")
        soft_step = sem("soft_step")
        shift_ready = sem("shift_ready")
        ex_ready = sem("ex_ready")
        cw_ready = sem("cw_ready")
        cwT_done = sem("cwT_done")
        cwT_ready = sem("cwT_ready")
        b2_done = sem("b2_done")
        b2_added = sem("b2_added")
        h_ready = sem("h_ready")
        gelu_done = sem("gelu_done")
        y_done = sem("y_done")
        y_weighed = sem("y_weighed")
        acc_done = sem("acc_done")

        wk_raw = prod[1][0:KR, 0:K * K * G]
        N_FEATURE = 3 + 1 + 1
        N_EXPERT = 3 + 2 + 2 + R

        block = ctx.enter_context(nc.Block())

        def image_rows(dram, row, bo, bi):
            return dram[2 * bo + bi, bass.ds(row, R), :, :].rearrange("h w c -> w h c")

        def half_rows(tile, bi):
            return tile[bi:T:2, :].rearrange("w (h c) -> w h c", c=C)

        def shifted(tile, r, j):
            lo = 2 * (r * WP + 2 * PAD - j)
            return tile[:, lo:lo + T]

        def interior(tile):
            return tile.rearrange("p (r w) -> p r w", w=2 * WP)[:, :, 2 * PAD:2 * PAD + T]

        @block.sync
        def _(sp):
            def at(value):
                return value if isinstance(value, int) else sp.snap(value)

            def load_x(row, bo):
                for bi in range(2):
                    sp.dma_start(half_rows(x_in[bo], bi), image_rows(x, row, bo, bi)).then_inc(x_in_loaded[bo], 16)

            def load_stage(q, bo):
                n = 2 * q + bo
                lo = at((bo * HP + PAD) * C + R * C * q)
                if some(n - 1):
                    sp.wait_ge(xt_done, n - 1)
                sp.dma_start(stage[bo][0:T, :], xn[0:T, bass.ds(lo, R * C)]) \
                    .then_inc(stage_loaded[bo], 16)

            def slot(q, bo):
                ql, bl = group(q, bo, 3)
                qx, bx = group(q, bo, 1)
                if exists(qx):
                    row = at(R * ql)
                    sp.wait_ge(xn_ready, 2 * q + bo + 2)
                if exists(ql):
                    load_x(row, bl)
                if exists(qx):
                    load_stage(qx, bx)
                qp, bp = group(q, bo, -1)
                if exists(qp):
                    n = 2 * qp + bp
                    row = at(R * qp)
                    if some(n - 1):
                        sp.wait_ge(t_done, n - 1)
                    for bi in range(2):
                        sp.dma_start(half_rows(x_res[bp], bi), image_rows(x, row, bp, bi)) \
                            .then_inc(x_res_loaded[bp], 16)
                qo, bo_ = group(q, bo, -2)
                if exists(qo):
                    store(qo, bo_)

            def load_weights():
                sp.dma_start(w1_raw[:, :].rearrange("p (e h) -> p e h", e=E), W1.rearrange("e d h -> d e h")) \
                    .then_inc(expert_in_sb, 16)
                sp.dma_start(gate_raw[:, :], gate_w).then_inc(expert_in_sb, 16)
                sp.dma_start(gate_bias[0:T, :].rearrange("p (r e) -> p r e", e=E),
                             gate_b.partition_broadcast(T).unsqueeze(1).to_broadcast([T, R, E])) \
                    .then_inc(expert_in_sb, 16)
                with nc.allow_non_contiguous_dma(reason="2048 bias values, once"):
                    for f in range(2):
                        sp.dma_start(b1_t[:, f:2 * E:2], b1[:, f * 128:(f + 1) * 128].rearrange("e p -> p e")) \
                            .then_inc(expert_in_sb, 16)
                for f in range(2):
                    sp.dma_start(w2_t[:, :].rearrange("p (e f c) -> p e f c", e=E, f=2)[:, :, f, :],
                                 W2[:, f * 128:(f + 1) * 128, :].rearrange("e p c -> p e c")) \
                        .then_inc(expert_in_sb, 16)
                sp.wait_ge(pool_const, 9)
                for r in range(R):
                    sp.dma_start(b2_rows[r * E:(r + 1) * E, r * C:(r + 1) * C], b2).then_inc(expert_in_sb, 16)

            def store(q, bo):
                row = at(R * q)
                sp.wait_ge(acc_done, E * (2 * q + bo + 1))
                for bi in (1, 0):
                    sp.dma_start(image_rows(out, row, bo, bi), half_rows(acc[bo], bi)).then_inc(out_stored[bo], 16)

            load_x(0, 0)
            for a in range(3):
                sp.dma_start(wk_raw[a * CR:(a + 1) * CR, :], w_span).then_inc(feature_in, 16)
            sp.dma_start(wk_raw[3 * CR:KR, :], b_span.partition_broadcast(2)).then_inc(feature_in, 16)
            sp.dma_start(wred3[:, :].rearrange("p (a d) -> p a d", a=3),
                         w_reduce.unsqueeze(1).to_broadcast([128, 3, CR])).then_inc(feature_in, 16)
            load_x(0, 1)
            sp.wait_ge(xn_ready, 1)
            load_x(R, 0)
            load_stage(0, 0)
            sp.wait_ge(wk_lo_ready, 1)
            sp.dma_start(wk[KR - 1:KR, :].bitcast(F32), wk_lo[KR - 1:KR, :].bitcast(F32)).then_inc(wk_row_in, 16)
            load_weights()

            for q in range(2):
                slot(q, 0)
                slot(q, 1)
            with sp.Fori(2, QN - 2) as q:
                slot(q, 0)
                slot(q, 1)
            for q in range(QN - 2, QN + 1):
                slot(q, 0)
                slot(q, 1)
            for bo in range(2):
                sp.wait_ge(out_stored[bo], 32 * QN)

        @block.gpsimd
        def _(pool):
            pool.memset(ident[:, :], 0.0).then_inc(pool_const, 1)
            pool.memset(minus_half[:, :], -0.5).then_inc(pool_const, 1)
            for i in range(2):
                pool.memset(rT[i][:, :].bitcast(F32), 0.0).then_inc(pool_const, 1)
            pool.memset(b2_rows[:, :], 0.0).then_inc(pool_const, 1)
            for bo in range(2):
                for top_row in (0, PAD + H):
                    lo = (bo * HP + top_row) * C
                    pool.memset(xn[0:T, lo:lo + PAD * C], 0.0).then_inc(pool_const, 1)
            pool.wait_ge(pool_const, 9)
            pool.affine_select(out=ident[:, :], in_=ident[:, :], compare_op=ALU.not_equal, fill=1.0, base=0,
                               pattern=[[-1, 128]], channel_multiplier=1).then_inc(pool_const, 1)
            pool.wait_ge(pool_const, 10)
            for i in range(2):
                pool.memset(rT[i][3 * CR:KR, :].bitcast(F32), 1.0).then_inc(pool_const, 1)
            pool.wait_ge(pool_const, 12)
            for e in range(E):
                pool.memset(expert_no[:, e:R * E:E], float(e)).then_inc(pool_const, 1)
            pool.wait_ge(bn_step, 2)
            nc.gpsimd.tensor_tensor(bn_rs[:, :], bn_ve[:, :], minus_half[0:3 * CR, 0:1], ALU.pow).then_inc(bn_pow, 1)

            def rstd(n, ve, nm, rs, nb, mv_ready, pow_done, ready, used):
                pool.wait_ge(mv_ready, 2 * n + 2)
                if some(n):
                    pool.wait_ge(used, n)
                nc.gpsimd.tensor_tensor(rs[0:T, :], ve[0:T, :], minus_half[0:T, :], ALU.pow).then_inc(pow_done, 1)
                pool.wait_ge(pow_done, n + 1)
                nc.gpsimd.tensor_tensor(nb[0:T, :], nm[0:T, :], rs[0:T, :], ALU.mult).then_inc(ready, 1)

            def rstd1(q, bo):
                rstd(2 * q + bo, ve1, nm1, rs1, nb1, mv1_ready, pow1_done, rstd1_ready, xn_ready)

            def feat_lo(q, bo):
                n = 2 * q + bo
                pool.wait_ge(feat_read, 2 * n + 2)
                inside = interior(rT[bo][2 * CR:3 * CR, :])
                nc.gpsimd.tensor_tensor(inside, r_lin[2 * CR:3 * CR, :].rearrange("p (r w) -> p r w", w=T),
                                        inside.bitcast(F32), ALU.subtract).then_inc(feat_ready, 1)
                pool.wait_ge(feat_ready, n + 1)

            def folds(q, bo, u):
                m = STEPS * (2 * q + bo) + u
                rows = prod[u % 4][0:T, :].rearrange("p (j i) -> p j i", i=ROWC)
                pool.wait_ge(prod_done, m + 1)
                nc.gpsimd.tensor_tensor(rows[:, :, 0:3 * C], rows[:, :, 0:3 * C], rows[:, :, 3 * C:6 * C],
                                        ALU.add).then_inc(fold_step if FOLDS[u % 2] > 1 else folds_done, 1)
                if FOLDS[u % 2] > 1:
                    fm = m + 1 if FOLDS == [2, 2] else STEPS // 2 * (2 * q + bo) + u // 2 + 1
                    pool.wait_ge(fold_step, fm)
                    nc.gpsimd.tensor_tensor(rows[:, :, 0:C], rows[:, :, 0:C], rows[:, :, 6 * C:7 * C],
                                            ALU.add).then_inc(folds_done, 1)

            def slot(q, bo):
                for u in range(STEPS):
                    if exists(q):
                        folds(q, bo, u)
                    qp, bp = group(q, bo, -1)
                    if u == 2 and exists(qp):
                        rstd(2 * qp + bp, ve2, nm2, rs2, nb2, mv2_ready, pow2_done, rstd2_ready, tn_ready)
                    ql, bl = group(q, bo, 3)
                    if u == 3 and exists(ql):
                        rstd1(ql, bl)
                    qx, bx = group(q, bo, 1)
                    if u == 4 and exists(qx):
                        pool.wait_ge(folds_done, STEPS * (2 * q + bo) + u + 1)
                        feat_lo(qx, bx)

            for d in range(3):
                rstd1(*group(0, 0, d))
                if d == 0:
                    pool.wait_ge(rstd1_ready, 1)
                    feat_lo(0, 0)
            for q in range(2):
                slot(q, 0)
                slot(q, 1)
            with pool.Fori(2, QN - 2) as q:
                slot(q, 0)
                slot(q, 1)
            for q in range(QN - 2, QN + 1):
                slot(q, 0)
                slot(q, 1)

        @block.scalar
        def _(act):
            for v, a in enumerate((gamma, beta, mean, var)):
                act.dma_start(bn_rows[v:v + 1, :].rearrange("o (a d) -> o a d", a=3),
                              a.unsqueeze(0).unsqueeze(0).to_broadcast([1, 3, CR])).then_inc(bn_rows_in, 16)

            def apply1(q, bo):
                n = 2 * q + bo
                act.wait_ge(rstd1_ready, n + 1)
                for r in range(R):
                    ins = act.activation(xn[0:T, bass.ds((bo * HP + PAD + r) * C + R * C * q, C)],
                                         x_in[bo][0:T, r * C:(r + 1) * C], ACT.Identity,
                                         bias=nb1[0:T, r:r + 1], scale=rs1[0:T, r:r + 1])
                ins.then_inc(xn_ready, 1)

            def take_xnT(q, bo):
                n = 2 * q + bo
                act.wait_ge(xt_done, n + 1)
                if some(n):
                    act.wait_ge(feat_done, n)
                act.activation(xnT[:, :], misc[:, 0:N], ACT.Copy).then_inc(xnT_ready, 1)

            def features(q, bo):
                n = 2 * q + bo
                act.wait_ge(feat_done, n + 1)
                if some(n - 1):
                    act.wait_ge(kg_ready, STEPS * (n - 1))
                if some(n):
                    act.wait_ge(feat_ready, n)
                act.activation(interior(rT[bo][0:3 * CR, :]),
                               misc[0:3 * CR, 0:N].rearrange("p (r w) -> p r w", w=T),
                               ACT.Relu, bias=bn_bias[:, :], scale=bn_scale[:, :]).then_inc(feat_read, 1)
                act.activation(r_lin[2 * CR:3 * CR, :], misc[2 * CR:3 * CR, 0:N], ACT.Relu,
                               bias=bn_bias[2 * CR:3 * CR, :], scale=bn_scale[2 * CR:3 * CR, :]) \
                    .then_inc(feat_read, 1)

            def take_conv(q, bo):
                n = 2 * q + bo
                act.wait_ge(conv_done, STEPS * (n + 1))
                if some(n):
                    act.wait_ge(back_done, n)
                act.activation(convT[:, :].rearrange("p (r w) -> p r w", w=T),
                               interior(conv_bank[:, 0:R * 2 * WP]), ACT.Copy).then_inc(convT_ready, 1)

            def apply2(q, bo):
                n = 2 * q + bo
                act.wait_ge(rstd2_ready, n + 1)
                if some(n):
                    act.wait_ge(tnT_done, n)
                for r in range(R):
                    ins = act.activation(tn[0:T, r * C:(r + 1) * C], t_row[0:T, r * C:(r + 1) * C], ACT.Identity,
                                         bias=nb2[0:T, r:r + 1], scale=rs2[0:T, r:r + 1])
                ins.then_inc(tn_ready, 1)

            def take_tn_hi(q, bo):
                n = 2 * q + bo
                act.wait_ge(tnT_done, n + 1)
                if some(n - 1):
                    act.wait_ge(h_ready, 2 * E * (n - 1))
                act.activation(tn_hi[bo][:, :], misc[:, 0:N], ACT.Copy).then_inc(tn_hi_ready, 1)

            def exps(q, bo):
                n = 2 * q + bo
                act.wait_ge(shift_ready, n + 1)
                if some(n):
                    act.wait_ge(cw_ready, n)
                act.activation(ex[0:T, :], lshift[0:T, :], ACT.Exp).then_inc(ex_ready, 1)

            def weigh(q, bo, e):
                m = E * (2 * q + bo) + e
                act.wait_ge(y_done, m + 1)
                if e == 0:
                    act.wait_ge(cw_ready, 2 * q + bo + 1)
                for r in range(R):
                    rows = y_bank[e % 2][0:T, r * C:(r + 1) * C]
                    ins = act.activation(rows, rows, ACT.Copy, scale=cw[bo][0:T, r * E + e:r * E + e + 1])
                ins.then_inc(y_weighed, 1)

            def gelus(q, bo, e):
                m = E * (2 * q + bo) + e
                for f in range(2):
                    act.wait_ge(h_ready, 2 * m + f + 1)
                    if some(m - 1):
                        act.wait_ge(y_done, m - 1)
                    act.activation(hT[e % 2][f][:, :], h_bank[f][:, 0:N], ACT.Gelu,
                                   bias=b1_t[:, 2 * e + f:2 * e + f + 1]).then_inc(gelu_done, 1)

            def slot(q, bo):
                for u in range(STEPS):
                    ql, bl = group(q, bo, 3)
                    qx, bx = group(q, bo, 1)
                    qp, bp = group(q, bo, -1)
                    if u == 6 and exists(qp):
                        exps(qp, bp)
                    qe, be, e = expert_at(q, bo, u, LAG_IN)
                    if exists(qe):
                        gelus(qe, be, e)
                    qe, be, e = expert_at(q, bo, u, LAG_ADD)
                    if exists(qe):
                        weigh(qe, be, e)
                    if u == 1 and exists(qx):
                        take_xnT(qx, bx)
                    if u == 1 and exists(qp):
                        take_conv(qp, bp)
                    if u == 3 and exists(qx):
                        features(qx, bx)
                    if u == 3 and exists(qp):
                        apply2(qp, bp)
                    if u == 4 and exists(qp):
                        take_tn_hi(qp, bp)
                    if u == 4 and exists(ql):
                        apply1(ql, bl)

            for d in range(3):
                apply1(*group(0, 0, d))
                if d == 0:
                    take_xnT(0, 0)
                    act.wait_ge(bn_ready, 2)
                    act.wait_ge(pool_const, 20)
                    features(0, 0)
            slot(0, 0)
            act.wait_ge(expert_in_sb, 16 * N_EXPERT)
            act.activation(w1_hi[:, :], w1_raw[:, :], ACT.Copy).then_inc(w1_hi_ready, 1)
            slot(0, 1)
            slot(1, 0)
            slot(1, 1)
            with act.Fori(2, QN - 2) as q:
                slot(q, 0)
                slot(q, 1)
            for q in range(QN - 2, QN + 1):
                slot(q, 0)
                slot(q, 1)

        @block.vector
        def _(dve):
            def moments(n, src, st, both, diff, var_in, sq, ve, nm, eps, step, ready, used):
                for r in range(R):
                    ins = dve.bn_stats(st[0:T, r, :], src[0:T, r * C:(r + 1) * C])
                ins.then_inc(step, 1)
                dve.wait_ge(step, 3 * n + 1)
                nc.vector.tensor_tensor(both[0:T], st[0:T, :, 0:3], st[0:T, :, 3:6], ALU.add)
                nc.vector.tensor_tensor(diff[0:T, :], st[0:T, :, 1], st[0:T, :, 4], ALU.subtract).then_inc(step, 1)
                dve.wait_ge(step, 3 * n + 2)
                if some(n):
                    dve.wait_ge(used, n)
                dve.tensor_scalar(nm[0:T, :], both[0:T, :, 1], -0.5, None, ALU.mult).then_inc(ready, 1)
                dve.tensor_scalar(var_in[0:T, :], both[0:T, :, 2], 1.0 / C, eps, ALU.mult, ALU.add)
                dve.scalar_tensor_tensor(out=sq[0:T, :], in0=diff[0:T, :], scalar=0.25, in1=diff[0:T, :],
                                         op0=ALU.mult, op1=ALU.mult).then_inc(step, 1)
                dve.wait_ge(step, 3 * n + 3)
                nc.vector.tensor_tensor(ve[0:T, :], var_in[0:T, :], sq[0:T, :], ALU.add).then_inc(ready, 1)

            def moments1(q, bo):
                dve.wait_ge(x_in_loaded[bo], 32 * q + 32)
                moments(2 * q + bo, x_in[bo], st1, *mv1, ve1, nm1, LN1_EPS, ln1_step, mv1_ready, rstd1_ready)

            def products(q, bo, u):
                m = STEPS * (2 * q + bo) + u
                r, half = u // 2, u % 2
                jn = JS[half][1]
                if u == 0:
                    qn, _ = group(q, bo, 2)
                    dve.wait_ge(xn_ready, 2 * q + bo + 3 if exists(qn) else 2 * QN)
                dve.wait_ge(kg_ready, m + 1)
                if some(m - 3):
                    dve.wait_ge(conv_done, m - 3)
                xs = xn[0:T, bass.ds((bo * HP + r) * C + R * C * q, ROWC)]
                xs = xs.rearrange("p (a b) -> p a b", b=CG).unsqueeze(1).to_broadcast([T, jn, K * G, CG])
                ks = kg_bank[half][0:T, 0:jn * K * G].rearrange("p (j a) -> p j a", j=jn)
                ks = ks.unsqueeze(3).to_broadcast([T, jn, K * G, CG])
                po = prod[u % 4][0:T, :].rearrange("p (j a b) -> p j a b", j=jn, b=CG)
                nc.vector.tensor_tensor(po, ks, xs, ALU.mult).then_inc(prod_done, 1)

            def add_expert(q, bo, e):
                m = E * (2 * q + bo) + e
                dve.wait_ge(y_weighed, m + 1)
                if e == 0 and some(q):
                    dve.wait_ge(out_stored[bo], 32 * q)
                if e == 0:
                    dve.wait_ge(t_done, 2 * q + bo + 1)
                else:
                    dve.wait_ge(acc_done, m)
                if e == 2:
                    dve.wait_ge(b2_added, 2 * q + bo + 1)
                nc.vector.tensor_tensor(acc[bo][0:T, :], y_bank[e % 2][0:T, :],
                                        (t_row if e == 0 else acc[bo])[0:T, :], ALU.add).then_inc(acc_done, 1)

            def add_b2(q, bo):
                n = 2 * q + bo
                dve.wait_ge(b2_done, n + 1)
                dve.wait_ge(acc_done, E * n + 2)
                nc.vector.tensor_tensor(acc[bo][0:T, :], misc[0:T, 0:R * C], acc[bo][0:T, :], ALU.add) \
                    .then_inc(b2_added, 1)

            def residual(q, bo):
                n = 2 * q + bo
                dve.wait_ge(back_done, n + 1)
                dve.wait_ge(x_res_loaded[bo], 32 * q + 32)
                if some(n):
                    dve.wait_ge(acc_done, E * (n - 1) + 1)
                    dve.wait_ge(tn_ready, n)
                nc.vector.tensor_tensor(t_row[0:T, :], misc[0:T, 0:R * C], x_res[bo][0:T, :], ALU.add) \
                    .then_inc(t_done, 1)
                dve.wait_ge(t_done, n + 1)
                moments(n, t_row, st2, *mv2, ve2, nm2, LN2_EPS, ln2_step, mv2_ready, rstd2_ready)

            def take_tn_lo(q, bo):
                dve.wait_ge(tn_hi_ready, 2 * q + bo + 1)
                nc.vector.tensor_tensor(tn_lo[bo][:, :], misc[:, 0:N], tn_hi[bo][:, :].bitcast(F32), ALU.subtract) \
                    .then_inc(tn_lo_ready, 1)

            def per_row(tile):
                return tile[0:T, :].rearrange("p (r e) -> p r e", e=E)

            def spread(tile):
                return tile.to_broadcast([T, R, E])

            SOFT = 9

            def shift_logits(q, bo):
                n = 2 * q + bo
                dve.wait_ge(gate_done, n + 1)
                nc.vector.tensor_tensor(logits[0:T, :], misc[0:T, 0:R * E], gate_bias[0:T, :], ALU.add) \
                    .then_inc(logits_read, 1)
                dve.wait_ge(logits_read, n + 1)
                dve.tensor_reduce(lmax[0:T, :], per_row(logits), AX.X, ALU.max).then_inc(soft_step, 1)
                dve.wait_ge(soft_step, SOFT * n + 1)
                if some(n):
                    dve.wait_ge(ex_ready, n)
                nc.vector.tensor_tensor(per_row(lshift), per_row(logits), spread(lmax[0:T, :].unsqueeze(2)),
                                        ALU.subtract).then_inc(shift_ready, 1)

            def top2_weights(q, bo):
                n = 2 * q + bo
                dve.wait_ge(ex_ready, n + 1)
                dve.tensor_reduce(esum[0:T, :], per_row(ex), AX.X, ALU.add).then_inc(soft_step, 1)
                for r in range(R):
                    ins = dve.max(top[0:T, r, :], ex[0:T, r * E:(r + 1) * E])
                ins.then_inc(soft_step, 1)
                dve.wait_ge(soft_step, SOFT * n + 3)
                dve.reciprocal(erec[0:T, :], esum[0:T, :]).then_inc(soft_step, 1)
                for r in range(R):
                    ins = dve.max_index(topi[0:T, r, :], top[0:T, r, :], ex[0:T, r * E:(r + 1) * E])
                ins.then_inc(soft_step, 1)
                dve.wait_ge(soft_step, SOFT * n + 5)
                for c, eq in enumerate((eq0, eq1)):
                    nc.vector.tensor_tensor(per_row(eq), per_row(expert_no), spread(topi[0:T, :, c:c + 1]),
                                            ALU.is_equal).then_inc(soft_step, 1)
                dve.wait_ge(soft_step, SOFT * n + 7)
                nc.vector.tensor_tensor(eqs[0:T, :], eq0[0:T, :], eq1[0:T, :], ALU.add).then_inc(soft_step, 1)
                nc.vector.tensor_tensor(per_row(exk), per_row(ex), spread(erec[0:T, :].unsqueeze(2)),
                                        ALU.mult).then_inc(soft_step, 1)
                dve.wait_ge(soft_step, SOFT * n + 9)
                nc.vector.tensor_tensor(cw[bo][0:T, :], exk[0:T, :], eqs[0:T, :], ALU.mult).then_inc(cw_ready, 1)

            def take_cwT(q, bo):
                n = 2 * q + bo
                dve.wait_ge(cwT_done, n + 1)
                if some(n):
                    dve.wait_ge(b2_done, n)
                dve.tensor_copy(cwT[:, :], misc[0:R * E, 0:T]).then_inc(cwT_ready, 1)

            def slot(q, bo):
                for u in range(STEPS):
                    if exists(q):
                        products(q, bo, u)
                    qe, be, e = expert_at(q, bo, u, LAG_ADD)
                    if exists(qe):
                        add_expert(qe, be, e)
                    qg, bg = group(q, bo, -2)
                    if u == 0 and exists(qg):
                        add_b2(qg, bg)
                    qp, bp = group(q, bo, -1)
                    ql, bl = group(q, bo, 3)
                    if u == 3 and exists(ql):
                        moments1(ql, bl)
                    if not exists(qp):
                        continue
                    if u == 2:
                        residual(qp, bp)
                    if u == 4:
                        take_tn_lo(qp, bp)
                    if u == 5:
                        shift_logits(qp, bp)
                    if u == 6:
                        top2_weights(qp, bp)
                    if u == 7:
                        take_cwT(qp, bp)

            moments1(0, 0)
            dve.wait_ge(bn_turned, 1)
            dve.tensor_copy(bn_in[:, :], kg_bank[1][0:3 * CR, 0:4]).then_inc(bn_step, 1)
            dve.wait_ge(bn_step, 1)
            dve.tensor_scalar(bn_ve[:, :], bn_in[:, 3:4], BN_EPS, None, ALU.add).then_inc(bn_step, 1)
            dve.wait_ge(feature_in, 16 * N_FEATURE)
            wk_order = wk_raw.rearrange("p (g i j) -> p j i g", g=G, i=K)
            for j in range(K):
                dve.tensor_copy(wk[:, j * K * G:(j + 1) * K * G].rearrange("p (i g) -> p i g", g=G),
                                wk_order[:, j, :, :]).then_inc(split_step, 1)
            dve.wait_ge(split_step, K)
            for j in range(K):
                part = slice(j * K * G, (j + 1) * K * G)
                ins = nc.vector.tensor_tensor(wk_lo[:, part].rearrange("p (i g) -> p i g", g=G), wk_order[:, j, :, :],
                                              wk[:, part].bitcast(F32).rearrange("p (i g) -> p i g", g=G),
                                              ALU.subtract)
            ins.then_inc(wk_lo_ready, 1)
            dve.wait_ge(wk_lo_ready, 1)
            dve.tensor_copy(wk[CR:2 * CR, :], wk_lo[CR:2 * CR, :].bitcast(F32)).then_inc(split_step, 1)
            dve.wait_ge(bn_pow, 1)
            nc.vector.tensor_tensor(bn_scale[:, :], bn_rs[:, :], bn_in[:, 0:1], ALU.mult).then_inc(bn_ready, 1)
            dve.wait_ge(bn_ready, 1)
            nc.vector.tensor_tensor(bn_ms[:, :], bn_scale[:, :], bn_in[:, 2:3], ALU.mult).then_inc(bn_step, 1)
            dve.wait_ge(bn_step, 3)
            nc.vector.tensor_tensor(bn_bias[:, :], bn_in[:, 1:2], bn_ms[:, :], ALU.subtract).then_inc(bn_ready, 1)
            moments1(0, 1)
            moments1(1, 0)
            dve.wait_ge(split_step, K + 1)
            dve.wait_ge(pool_const, 20)
            slot(0, 0)
            dve.wait_ge(expert_in_sb, 16 * N_EXPERT)
            dve.tensor_copy(gate_hi[:, :], gate_raw[:, :]).then_inc(split_step, 1)
            dve.wait_ge(w1_hi_ready, 1)
            nc.vector.tensor_tensor(w1_lo[:, :], w1_raw[:, :], w1_hi[:, :].bitcast(F32), ALU.subtract) \
                .then_inc(experts_split, 1)
            dve.wait_ge(split_step, K + 2)
            nc.vector.tensor_tensor(gate_lo[:, :], gate_raw[:, :], gate_hi[:, :].bitcast(F32), ALU.subtract) \
                .then_inc(experts_split, 1)
            slot(0, 1)
            slot(1, 0)
            slot(1, 1)
            with dve.Fori(2, QN - 2) as q:
                slot(q, 0)
                slot(q, 1)
            for q in range(QN - 2, QN + 1):
                slot(q, 0)
                slot(q, 1)

        @block.tensor
        def _(pe):
            ident_row = ident[0:T, 0:T]

            def transpose_in(q, bo):
                n = 2 * q + bo
                pe.wait_ge(stage_loaded[bo], 16 * q + 16)
                if some(n):
                    pe.wait_ge(feat_read, 2 * n)
                if some(n - 2):
                    pe.wait_ge(b2_added, n - 2)
                for r in range(R):
                    mm = pe.transpose(misc[:, r * T:(r + 1) * T], stage[bo][0:T, r * C:(r + 1) * C], ident_row)
                mm.then_inc(xt_done, 1)

            def reduce_channels(q, bo):
                n = 2 * q + bo
                pe.wait_ge(xnT_ready, n + 1)
                if some(n - 1):
                    pe.wait_ge(t_done, n - 1)
                pe.matmul(misc[0:3 * CR, 0:N], wred3[:, :], xnT[:, :], start=True, stop=True) \
                    .then_inc(feat_done, 1)

            def kernels(q, bo, u):
                m = STEPS * (2 * q + bo) + u
                r, half = u // 2, u % 2
                if u == 0:
                    pe.wait_ge(feat_ready, 2 * q + bo + 1)
                if some(m - 1):
                    pe.wait_ge(prod_done, m - 1)
                j0, jn = JS[half]
                for j in range(j0, j0 + jn):
                    mm = pe.matmul(kg_bank[half][0:T, (j - j0) * K * G:(j - j0 + 1) * K * G],
                                   shifted(rT[bo], r, j), wk[:, j * K * G:(j + 1) * K * G],
                                   start=True, stop=True)
                mm.then_inc(kg_ready, 1)

            def gather_taps(q, bo, u):
                m = STEPS * (2 * q + bo) + u
                r, half = u // 2, u % 2
                pe.wait_ge(folds_done, m + 1)
                if u == 0 and some(2 * q + bo):
                    pe.wait_ge(convT_ready, 2 * q + bo)
                j0, jn = JS[half]
                kept = [0, 1, 2] if FOLDS[half] > 1 else [0, 1, 2, 6]
                for j in range(j0, j0 + jn):
                    for i in kept:
                        at = (j - j0) * ROWC + i * C
                        mm = pe.matmul(shifted(conv_bank, r, j), prod[u % 4][0:T, at:at + C],
                                       ident_row, is_transpose=True,
                                       start=(u == 0 and j == j0 and i == 0),
                                       stop=(u == STEPS - 1 and j == K - 1 and i == kept[-1]),
                                       skip_group_check=True)
                mm.then_inc(conv_done, 1)

            def transpose_back(q, bo):
                n = 2 * q + bo
                qx, _ = group(q, bo, 2)
                pe.wait_ge(convT_ready, n + 1)
                if exists(qx):
                    pe.wait_ge(xnT_ready, n + 3)
                else:
                    pe.wait_ge(b2_added, n)
                for r in range(R):
                    mm = pe.transpose(misc[0:T, r * C:(r + 1) * C], convT[:, r * T:(r + 1) * T], ident[:, :])
                mm.then_inc(back_done, 1)

            def transpose_tn(q, bo):
                n = 2 * q + bo
                qx, _ = group(q, bo, 2)
                pe.wait_ge(tn_ready, n + 1)
                if exists(qx):
                    pe.wait_ge(feat_read, 2 * n + 6)
                for r in range(R):
                    mm = pe.transpose(misc[:, r * T:(r + 1) * T], tn[0:T, r * C:(r + 1) * C], ident_row)
                mm.then_inc(tnT_done, 1)

            def gate(q, bo):
                pe.wait_ge(tn_lo_ready, 2 * q + bo + 1)
                for r in range(R):
                    at = slice(r * T, (r + 1) * T)
                    to = misc[0:T, r * E:(r + 1) * E]
                    pe.matmul(to, tn_hi[bo][:, at], gate_hi[:, :], start=True, stop=False)
                    pe.matmul(to, tn_hi[bo][:, at], gate_lo[:, :], start=False, stop=False)
                    mm = pe.matmul(to, tn_lo[bo][:, at], gate_hi[:, :], start=False, stop=True)
                mm.then_inc(gate_done, 1)

            def transpose_cw(q, bo):
                n = 2 * q + bo
                pe.wait_ge(cw_ready, n + 1)
                pe.wait_ge(logits_read, n + 1)
                pe.transpose(misc[0:R * E, 0:T], cw[bo][0:T, :], ident_row).then_inc(cwT_done, 1)

            def expert_bias(q, bo):
                pe.wait_ge(cwT_ready, 2 * q + bo + 1)
                for r in range(R):
                    mm = pe.matmul(misc[0:T, r * C:(r + 1) * C], cwT[:, :], b2_rows[:, r * C:(r + 1) * C],
                                   start=True, stop=True)
                mm.then_inc(b2_done, 1)

            def expert_in(q, bo, e):
                m = E * (2 * q + bo) + e
                if e == 0:
                    pe.wait_ge(tn_lo_ready, 2 * q + bo + 1)
                for f in range(2):
                    if some(m):
                        pe.wait_ge(gelu_done, 2 * m - 1 + f)
                    at = slice(e * HID + f * 128, e * HID + (f + 1) * 128)
                    to = h_bank[f][:, 0:N]
                    pe.matmul(to, w1_hi[:, at], tn_hi[bo][:, :], start=True, stop=False)
                    pe.matmul(to, w1_hi[:, at], tn_lo[bo][:, :], start=False, stop=False)
                    pe.matmul(to, w1_lo[:, at], tn_hi[bo][:, :], start=False, stop=True).then_inc(h_ready, 1)

            def expert_out(q, bo, e):
                m = E * (2 * q + bo) + e
                pe.wait_ge(gelu_done, 2 * m + 2)
                if some(m - 1):
                    pe.wait_ge(acc_done, m - 1)
                for r in range(R):
                    for f in range(2):
                        mm = pe.matmul(y_bank[e % 2][0:T, r * C:(r + 1) * C], hT[e % 2][f][:, r * T:(r + 1) * T],
                                       w2_t[:, (2 * e + f) * C:(2 * e + f + 1) * C], start=(f == 0), stop=(f == 1))
                mm.then_inc(y_done, 1)

            def slot(q, bo):
                qx, bx = group(q, bo, 1)
                qp, bp = group(q, bo, -1)
                qg, bg = group(q, bo, -2)
                for u in range(STEPS):
                    qk, bk = (q, bo) if u < STEPS - 1 else (qx, bx)
                    if exists(qk):
                        kernels(qk, bk, (u + 1) % STEPS)
                    qe, be, e = expert_at(q, bo, u, LAG_IN)
                    if exists(qe):
                        expert_in(qe, be, e)
                    if u == 0 and exists(qg):
                        expert_bias(qg, bg)
                    if u == 1 and exists(qx):
                        transpose_in(qx, bx)
                    if u == 2 and exists(qp):
                        transpose_back(qp, bp)
                    if u == 3 and exists(qx):
                        reduce_channels(qx, bx)
                    if u == 4 and exists(qp):
                        transpose_tn(qp, bp)
                    if u == 5 and exists(qp):
                        gate(qp, bp)
                    if u == 7 and exists(qp):
                        transpose_cw(qp, bp)
                    qc, bc = (qp, bp) if u < 2 else (q, bo)
                    if exists(qc):
                        gather_taps(qc, bc, (u - 2) % STEPS)
                    qe, be, e = expert_at(q, bo, u, LAG_OUT)
                    if exists(qe):
                        expert_out(qe, be, e)

            pe.wait_ge(pool_const, 20)
            pe.wait_ge(bn_rows_in, 16 * 4)
            pe.transpose(kg_bank[1][0:3 * CR, 0:4], bn_rows[:, :], ident[0:4, 0:4]).then_inc(bn_turned, 1)
            transpose_in(0, 0)
            pe.wait_ge(feature_in, 16 * N_FEATURE)
            reduce_channels(0, 0)
            pe.wait_ge(split_step, K + 1)
            pe.wait_ge(wk_row_in, 16)
            kernels(0, 0, 0)
            slot(0, 0)
            pe.wait_ge(expert_in_sb, 16 * N_EXPERT)
            pe.wait_ge(experts_split, 2)
            slot(0, 1)
            slot(1, 0)
            slot(1, 1)
            with pe.Fori(2, QN - 2) as q:
                slot(q, 0)
                slot(q, 1)
            for q in range(QN - 2, QN + 1):
                slot(q, 0)
                slot(q, 1)


_INS = ['x', 'L0_conv_w_reduce', 'L0_conv_gamma', 'L0_conv_beta', 'L0_conv_mean', 'L0_conv_var', 'L0_conv_w_span',
        'L0_conv_b_span', 'L0_ffn_gate_w', 'L0_ffn_gate_b', 'L0_ffn_W1', 'L0_ffn_b1', 'L0_ffn_W2', 'L0_ffn_b2']
_OUTS = [((4, 56, 56, 128), 'float32')]


def kernel(**inputs):
    import numpy as _np
    import concourse.bacc as _bacc
    from concourse import mybir as _mybir
    from concourse.bass_utils import run_bass_kernel_spmd as _run

    nc = _bacc.Bacc("TRN2", target_bir_lowering=False, num_devices=1)
    arrays, args = {}, []
    for name in _INS:
        a = _np.ascontiguousarray(inputs[name])
        arrays[f"in_{name}_dram"] = a
        args.append(nc.dram_tensor(f"in_{name}_dram", a.shape, _mybir.dt.from_np(a.dtype), kind="ExternalInput").ap())
    for i, (shape, dtype) in enumerate(_OUTS):
        dt = _mybir.dt.from_np(_np.dtype(dtype))
        args.append(nc.dram_tensor(f"out_{i}_dram", shape, dt, kind="ExternalOutput").ap())
    metaformer_kernel(nc, *args)
    r = _run(nc, [arrays], core_ids=[0])
    got = tuple(r.results[0][f"out_{i}_dram"] for i in range(len(_OUTS)))
    return got[0]
```

```python
from contextlib import ExitStack

import concourse.bass as bass
from concourse import mybir

F32 = mybir.dt.float32
F32R = mybir.dt.float32r
U32 = mybir.dt.uint32
ALU = mybir.AluOpType
ACT = mybir.ActivationFunctionType
AX = mybir.AxisListType


def metaformer_kernel(nc, x, w_reduce, gamma, beta, mean, var, w_span, b_span,
                      gate_w, gate_b, W1, b1, W2, b2, out):
    B, H, W, C = x.shape
    CR = w_reduce.shape[1]
    E = gate_w.shape[1]
    HID = W1.shape[2]
    K = 7
    PAD = K // 2
    G = w_span.shape[1] // (K * K)
    CG = C // G
    assert B == 4 and C == 128 and CR == 32 and HID == 2 * 128
    T = 2 * W
    R = 4
    N = R * T
    QN = H // R
    STEPS = 2 * R
    assert STEPS == E
    WP = W + 2 * PAD
    HP = H + 2 * PAD
    JS = [(0, 4), (4, 3)]
    DEEP = [0, 1, 2, 3, 4, 6, 7]
    PLAIN = 2
    THIN = [1, 4]
    ROWC = K * C
    KR = 3 * CR + 2
    LN1_EPS, LN2_EPS, BN_EPS = 1e-6, 1e-5, 1e-3
    LAG_IN, LAG_OUT, LAG_WEIGH, LAG_ADD = 14, 15, 16, 17
    B2_WITH = 2

    def group(q, bo, d):
        return q + (bo + d) // 2, (bo + d) % 2

    def expert_at(q, bo, u, lag):
        d, e = divmod(u - lag, STEPS)
        return (*group(q, bo, d), e)

    def in_place(q):
        return isinstance(q, int) and q == 0

    def plain(q):
        return isinstance(q, int) and 2 * q < PLAIN

    def exists(q):
        return not isinstance(q, int) or 0 <= q < QN

    def some(value):
        return not isinstance(value, int) or value > 0

    ctx = ExitStack()
    with ctx:
        def sb(name, shape, dt=F32):
            return ctx.enter_context(nc.sbuf_tensor(name, shape, dt))

        def bank(name):
            return ctx.enter_context(nc.psum_tensor(name, [128, 512], F32))

        def sem(name):
            return ctx.enter_context(nc.semaphore(name))

        ident = sb("ident", [128, 128])
        minus_half = sb("minus_half", [128, R])
        wred3 = sb("wred3", [128, 3 * CR])
        bn_rows = sb("bn_rows", [4, 3 * CR])
        bn_in = sb("bn_in", [3 * CR, 4])
        bn_ve = sb("bn_ve", [3 * CR, 1])
        bn_rs = sb("bn_rs", [3 * CR, 1])
        bn_scale = sb("bn_scale", [3 * CR, 1])
        bn_ms = sb("bn_ms", [3 * CR, 1])
        bn_bias = sb("bn_bias", [3 * CR, 1])
        wk = sb("wk", [KR, K * K * G], F32R)
        wk_lo = sb("wk_lo", [KR, K * K * G], F32R)
        w1_raw = sb("w1_raw", [128, E * HID])
        w1_hi = sb("w1_hi", [128, E * HID], F32R)
        w1_lo = sb("w1_lo", [128, E * HID], F32R)
        b1_t = sb("b1_t", [128, E * 2])
        w2_t = sb("w2_t", [128, E * 2 * C])
        b2_raw = sb("b2_raw", [3 * R * E, R * C])
        b2_rows = sb("b2_rows", [3 * R * E, R * C], F32R)
        gate_raw = sb("gate_raw", [128, E])
        gate_parts = sb("gate_parts", [128, 2 * E], F32R)
        gate_bias = sb("gate_bias", [128, R * E])
        expert_no = sb("expert_no", [128, R * E])
        unread = sb("unread", [128, R * C])
        x_in = [sb(f"x_in{i}", [128, R * C]) for i in range(2)]
        sum1 = sb("sum1", [128, R])
        sqs1 = sb("sqs1", [128, R])
        ve1 = sb("ve1", [128, R])
        nm1 = sb("nm1", [128, R])
        rs1 = sb("rs1", [128, R])
        nb1 = sb("nb1", [128, R])
        xn = sb("xn", [128, 2 * HP * C])
        first = {name: sb(f"first_{name}", [128, 3 * R]) for name in ("diff", "nm", "var_in", "sq", "ve", "rs", "nb")}
        stage = [sb(f"stage{i}", [128, R * C]) for i in range(2)]
        xnT = sb("xnT", [128, N])
        r_lin = sb("r_lin", [128, N])
        rT = [sb(f"rT{i}", [KR, R * 2 * WP], F32R) for i in range(2)]
        prod = [sb(f"prod{i}", [128, JS[i % 2][1] * ROWC]) for i in range(4)]
        convT = sb("convT", [128, N])
        x_res = [sb(f"x_res{i}", [128, R * C]) for i in range(2)]
        t_row = sb("t_row", [128, R * C])
        sum2 = sb("sum2", [128, R])
        sqs2 = sb("sqs2", [128, R])
        ve2 = sb("ve2", [128, R])
        nm2 = sb("nm2", [128, R])
        rs2 = sb("rs2", [128, R])
        nb2 = sb("nb2", [128, R])
        tn = sb("tn", [128, R * C])
        tn_hi = [sb(f"tn_hi{i}", [128, N], F32R) for i in range(2)]
        tn_lo = [sb(f"tn_lo{i}", [128, N], F32R) for i in range(2)]
        logits_part = sb("logits_part", [128, R * E])
        neg_logits = sb("neg_logits", [128, R * E])
        neg_max = sb("neg_max", [128, R])
        ex = sb("ex", [128, R * E])
        esum = sb("esum", [128, R])
        erec = sb("erec", [128, R])
        top = sb("top", [128, R, 8])
        topi = sb("topi", [128, R, 8], U32)
        eq0 = sb("eq0", [128, R * E])
        eq1 = sb("eq1", [128, R * E])
        eqs = sb("eqs", [128, R * E])
        exk = sb("exk", [128, R * E])
        cw = [sb(f"cw{i}", [128, 3 * R * E]) for i in range(2)]
        cwT = sb("cwT", [3 * R * E, T], F32R)
        hT = [[sb(f"hT{i}{f}", [128, N]) for f in range(2)] for i in range(2)]
        weighed = [sb(f"weighed{i}", [128, R * C]) for i in range(2)]
        acc = [sb(f"acc{i}", [128, R * C]) for i in range(2)]

        kg_bank = [bank("kg0"), bank("kg1")]
        conv_bank = bank("conv")
        misc = bank("misc")
        h_bank = [bank("h0"), bank("h1")]
        y_bank = [bank("y0"), bank("y1")]

        feature_in = sem("feature_in")
        bn_rows_in = sem("bn_rows_in")
        bn_turned = sem("bn_turned")
        expert_in_sb = sem("expert_in_sb")
        wk_row_in = sem("wk_row_in")
        x_in_loaded = [sem(f"x_in_loaded{i}") for i in range(2)]
        stage_loaded = [sem(f"stage_loaded{i}") for i in range(2)]
        x_res_loaded = [sem(f"x_res_loaded{i}") for i in range(2)]
        out_stored = [sem(f"out_stored{i}") for i in range(2)]
        pool_const = sem("pool_const")
        bn_step = sem("bn_step")
        bn_pow = sem("bn_pow")
        bn_ready = sem("bn_ready")
        split_step = sem("split_step")
        wk_lo_ready = sem("wk_lo_ready")
        hi_ready = sem("hi_ready")
        experts_split = sem("experts_split")
        first_x_loaded = [sem(f"first_x_loaded{i}") for i in range(3)]
        first_step = sem("first_step")
        first_ve_ready = sem("first_ve_ready")
        first_pow = sem("first_pow")
        first_rstd_ready = sem("first_rstd_ready")
        ln1_step = sem("ln1_step")
        ve1_ready = sem("ve1_ready")
        pow1_done = sem("pow1_done")
        rstd1_ready = sem("rstd1_ready")
        xn_ready = sem("xn_ready")
        xt_done = sem("xt_done")
        xnT_ready = sem("xnT_ready")
        feat_done = sem("feat_done")
        feat_read = sem("feat_read")
        feat_ready = sem("feat_ready")
        kg_ready = sem("kg_ready")
        prod_done = sem("prod_done")
        thin_done = sem("thin_done")
        fold_step = sem("fold_step")
        folds_done = sem("folds_done")
        conv_done = sem("conv_done")
        convT_ready = sem("convT_ready")
        back_done = sem("back_done")
        t_done = sem("t_done")
        ln2_step = sem("ln2_step")
        ve2_ready = sem("ve2_ready")
        pow2_done = sem("pow2_done")
        rstd2_ready = sem("rstd2_ready")
        tn_ready = sem("tn_ready")
        tnT_done = sem("tnT_done")
        tn_hi_ready = sem("tn_hi_ready")
        tn_lo_ready = sem("tn_lo_ready")
        gate_done = sem("gate_done")
        logits_read = sem("logits_read")
        soft_step = sem("soft_step")
        max_ready = sem("max_ready")
        ex_ready = sem("ex_ready")
        cw_ready = sem("cw_ready")
        cwT_done = sem("cwT_done")
        cwT_hi_ready = sem("cwT_hi_ready")
        cwT_ready = sem("cwT_ready")
        b2_in = sem("b2_in")
        b2_done = sem("b2_done")
        h_ready = sem("h_ready")
        gelu_done = sem("gelu_done")
        y_done = sem("y_done")
        y_weighed = sem("y_weighed")
        acc_done = sem("acc_done")

        FIRST = [(0, 0), (1, 0), (0, 1)]
        first_x = [x_in[0], prod[2], x_in[1]]
        first_st = prod[3][:, 0:3 * R * 6].rearrange("p (r m) -> p r m", m=6)
        first_both = prod[3][:, 3 * R * 6:3 * R * 9].rearrange("p (r m) -> p r m", m=3)
        wk_raw = prod[1][0:KR, 0:K * K * G]
        N_FEATURE = 3 + 1 + 1
        N_EXPERT = 3 + 2 + 2

        block = ctx.enter_context(nc.Block())

        def image_rows(dram, row, bo, bi):
            return dram[2 * bo + bi, bass.ds(row, R), :, :].rearrange("h w c -> w h c")

        def half_rows(tile, bi):
            return tile[bi:T:2, :].rearrange("w (h c) -> w h c", c=C)

        def shifted(tile, r, j):
            lo = 2 * (r * WP + 2 * PAD - j)
            return tile[:, lo:lo + T]

        def interior(tile):
            return tile.rearrange("p (r w) -> p r w", w=2 * WP)[:, :, 2 * PAD:2 * PAD + T]

        @block.sync
        def _(sp):
            def at(value):
                return value if isinstance(value, int) else sp.snap(value)

            def load_x(row, bo):
                for bi in range(2):
                    sp.dma_start(half_rows(x_in[bo], bi), image_rows(x, row, bo, bi)).then_inc(x_in_loaded[bo], 16)

            def load_first(k):
                q, bo = FIRST[k]
                for bi in range(2):
                    sp.dma_start(half_rows(first_x[k][:, 0:R * C], bi), image_rows(x, R * q, bo, bi)) \
                        .then_inc(first_x_loaded[k], 16)

            def load_stage(q, bo):
                n = 2 * q + bo
                lo = at((bo * HP + PAD) * C + R * C * q)
                if some(n - 1):
                    sp.wait_ge(xt_done, n - 1)
                sp.dma_start(stage[bo][0:T, :], xn[0:T, bass.ds(lo, R * C)]) \
                    .then_inc(stage_loaded[bo], 16)

            def slot(q, bo):
                ql, bl = group(q, bo, 3)
                qx, bx = group(q, bo, 1)
                if exists(qx):
                    row = at(R * ql)
                    sp.wait_ge(xn_ready, max(3, 2 * q + bo + 2) if isinstance(q, int) else 2 * q + bo + 2)
                if exists(ql):
                    load_x(row, bl)
                if exists(qx) and not in_place(qx):
                    load_stage(qx, bx)
                qp, bp = group(q, bo, -1)
                if exists(qp):
                    n = 2 * qp + bp
                    row = at(R * qp)
                    if some(n - 1):
                        sp.wait_ge(t_done, n - 1)
                    for bi in range(2):
                        sp.dma_start(half_rows(x_res[bp], bi), image_rows(x, row, bp, bi)) \
                            .then_inc(x_res_loaded[bp], 16)
                qo, bo_ = group(q, bo, -3)
                if exists(qo):
                    store(qo, bo_)

            def load_weights():
                sp.dma_start(w1_raw[:, :].rearrange("p (e h) -> p e h", e=E), W1.rearrange("e d h -> d e h")) \
                    .then_inc(expert_in_sb, 16)
                sp.dma_start(gate_raw[:, :], gate_w).then_inc(expert_in_sb, 16)
                sp.dma_start(gate_bias[0:T, :].rearrange("p (r e) -> p r e", e=E),
                             gate_b.partition_broadcast(T).unsqueeze(1).to_broadcast([T, R, E])) \
                    .then_inc(expert_in_sb, 16)
                with nc.allow_non_contiguous_dma(reason="2048 bias values, once"):
                    for f in range(2):
                        sp.dma_start(b1_t[:, f:2 * E:2], b1[:, f * 128:(f + 1) * 128].rearrange("e p -> p e")) \
                            .then_inc(expert_in_sb, 16)
                for f in range(2):
                    sp.dma_start(w2_t[:, :].rearrange("p (e f c) -> p e f c", e=E, f=2)[:, :, f, :],
                                 W2[:, f * 128:(f + 1) * 128, :].rearrange("e p c -> p e c")) \
                        .then_inc(expert_in_sb, 16)
                sp.wait_ge(pool_const, 9)
                for a in range(3):
                    for r in range(R):
                        sp.dma_start(b2_raw[(a * R + r) * E:(a * R + r + 1) * E, r * C:(r + 1) * C], b2) \
                            .then_inc(b2_in, 16)

            def store(q, bo):
                row = at(R * q)
                sp.wait_ge(acc_done, E * (2 * q + bo + 1))
                for bi in (1, 0):
                    sp.dma_start(image_rows(out, row, bo, bi), half_rows(acc[bo], bi)).then_inc(out_stored[bo], 16)

            load_first(0)
            load_first(1)
            for a in range(3):
                sp.dma_start(wk_raw[a * CR:(a + 1) * CR, :], w_span).then_inc(feature_in, 16)
            sp.dma_start(wk_raw[3 * CR:KR, :], b_span.partition_broadcast(2)).then_inc(feature_in, 16)
            sp.dma_start(wred3[:, :].rearrange("p (a d) -> p a d", a=3),
                         w_reduce.unsqueeze(1).to_broadcast([128, 3, CR])).then_inc(feature_in, 16)
            load_first(2)
            sp.wait_ge(wk_lo_ready, 1)
            sp.dma_start(wk[KR - 1:KR, :].bitcast(F32), wk_lo[KR - 1:KR, :].bitcast(F32)).then_inc(wk_row_in, 16)
            load_weights()

            for q in range(2):
                slot(q, 0)
                slot(q, 1)
            with sp.Fori(2, QN - 2) as q:
                slot(q, 0)
                slot(q, 1)
            for q in range(QN - 2, QN + 1):
                slot(q, 0)
                slot(q, 1)
            store(QN - 1, 1)
            for bo in range(2):
                sp.wait_ge(out_stored[bo], 32 * QN)

        @block.gpsimd
        def _(pool):
            pool.memset(ident[:, :], 0.0).then_inc(pool_const, 1)
            pool.memset(minus_half[:, :], -0.5).then_inc(pool_const, 1)
            for i in range(2):
                pool.memset(rT[i][:, :].bitcast(F32), 0.0).then_inc(pool_const, 1)
            pool.memset(b2_raw[:, :], 0.0).then_inc(pool_const, 1)
            for bo in range(2):
                for top_row in (0, PAD + H):
                    lo = (bo * HP + top_row) * C
                    pool.memset(xn[0:T, lo:lo + PAD * C], 0.0).then_inc(pool_const, 1)
            pool.wait_ge(pool_const, 9)
            pool.affine_select(out=ident[:, :], in_=ident[:, :], compare_op=ALU.not_equal, fill=1.0, base=0,
                               pattern=[[-1, 128]], channel_multiplier=1).then_inc(pool_const, 1)
            pool.wait_ge(pool_const, 10)
            for i in range(2):
                pool.memset(rT[i][3 * CR:KR, :].bitcast(F32), 1.0).then_inc(pool_const, 1)
            pool.wait_ge(pool_const, 12)
            for e in range(E):
                pool.memset(expert_no[:, e:R * E:E], float(e)).then_inc(pool_const, 1)

            def rstd_first(k):
                at = slice(k * R, (k + 1) * R)
                pool.wait_ge(first_ve_ready, k + 1)
                nc.gpsimd.tensor_tensor(first["rs"][0:T, at], first["ve"][0:T, at], minus_half[0:T, :], ALU.pow) \
                    .then_inc(first_pow, 1)
                pool.wait_ge(first_pow, k + 1)
                nc.gpsimd.tensor_tensor(first["nb"][0:T, at], first["nm"][0:T, at], first["rs"][0:T, at],
                                        ALU.mult).then_inc(first_rstd_ready, 1)

            def rstd(n, ve, nm, rs, nb, ve_ready, pow_done, ready, used):
                pool.wait_ge(ve_ready, n + 1)
                if some(n):
                    pool.wait_ge(*used)
                nc.gpsimd.tensor_tensor(rs[0:T, :], ve[0:T, :], minus_half[0:T, :], ALU.pow).then_inc(pow_done, 1)
                pool.wait_ge(pow_done, n + 1)
                nc.gpsimd.tensor_tensor(nb[0:T, :], nm[0:T, :], rs[0:T, :], ALU.mult).then_inc(ready, 1)

            def rstd1(q, bo):
                n = 2 * q + bo
                rstd(n - 3, ve1, nm1, rs1, nb1, ve1_ready, pow1_done, rstd1_ready, (xn_ready, n))

            def feat_lo(q, bo):
                n = 2 * q + bo
                pool.wait_ge(feat_read, 2 * n + 2)
                inside = interior(rT[bo][2 * CR:3 * CR, :])
                nc.gpsimd.tensor_tensor(inside, r_lin[2 * CR:3 * CR, :].rearrange("p (r w) -> p r w", w=T),
                                        inside.bitcast(F32), ALU.subtract).then_inc(feat_ready, 1)
                pool.wait_ge(feat_ready, n + 1)

            def folds(q, bo, u):
                m = STEPS * (2 * q + bo) + u
                n = 2 * q + bo - PLAIN
                rows = prod[u % 4][0:T, :].rearrange("p (j i) -> p j i", i=ROWC)
                if u in THIN:
                    pool.wait_ge(thin_done, len(THIN) * n + THIN.index(u) + 1)
                else:
                    pool.wait_ge(prod_done, m + 1)
                nc.gpsimd.tensor_tensor(rows[:, :, 0:3 * C], rows[:, :, 0:3 * C], rows[:, :, 3 * C:6 * C],
                                        ALU.add).then_inc(fold_step if u in DEEP else folds_done, 1)
                if u not in DEEP:
                    return
                pool.wait_ge(fold_step, len(DEEP) * n + DEEP.index(u) + 1)
                tap = 1 if u in THIN else 6
                nc.gpsimd.tensor_tensor(rows[:, :, 0:C], rows[:, :, 0:C], rows[:, :, tap * C:(tap + 1) * C],
                                        ALU.add).then_inc(folds_done, 1)

            def slot(q, bo):
                for u in range(STEPS):
                    if exists(q) and not plain(q):
                        folds(q, bo, u)
                    qp, bp = group(q, bo, -1)
                    if u == 2 and exists(qp):
                        rstd(2 * qp + bp, ve2, nm2, rs2, nb2, ve2_ready, pow2_done, rstd2_ready, (tn_ready, 2 * qp + bp))
                    ql, bl = group(q, bo, 3)
                    qx, bx = group(q, bo, 1)
                    if u == 5 and exists(qx):
                        if plain(q):
                            pool.wait_ge(rstd1_ready, 2 * q + bo + 1)
                        else:
                            pool.wait_ge(folds_done, STEPS * (2 * q + bo - PLAIN) + u + 1)
                        feat_lo(qx, bx)
                    if u == 3 and exists(ql):
                        rstd1(ql, bl)

            rstd_first(0)
            pool.wait_ge(first_rstd_ready, 1)
            pool.wait_ge(bn_step, 2)
            nc.gpsimd.tensor_tensor(bn_rs[:, :], bn_ve[:, :], minus_half[0:3 * CR, 0:1], ALU.pow).then_inc(bn_pow, 1)
            pool.wait_ge(bn_pow, 1)
            rstd_first(1)
            pool.wait_ge(first_rstd_ready, 2)
            feat_lo(0, 0)
            pool.wait_ge(feat_ready, 1)
            rstd_first(2)
            slot(0, 0)
            for no, (lo, raw, hi) in enumerate(((w1_lo, w1_raw, w1_hi), (gate_parts[:, E:2 * E], gate_raw, gate_parts[:, 0:E]))):
                pool.wait_ge(hi_ready, no + 1)
                nc.gpsimd.tensor_tensor(lo[:, :], raw[:, :], hi[:, :].bitcast(F32), ALU.subtract) \
                    .then_inc(experts_split, 1)
            pool.wait_ge(experts_split, 2)
            slot(0, 1)
            pool.wait_ge(feat_ready, 3)
            pool.wait_ge(hi_ready, 3)
            part = slice(2 * R * E, 3 * R * E)
            nc.gpsimd.tensor_tensor(b2_rows[part, :], b2_raw[part, :], b2_rows[part, :].bitcast(F32), ALU.subtract) \
                .then_inc(experts_split, 1)
            pool.wait_ge(experts_split, 3)
            slot(1, 0)
            slot(1, 1)
            with pool.Fori(2, QN - 2) as q:
                slot(q, 0)
                slot(q, 1)
            for q in range(QN - 2, QN + 1):
                slot(q, 0)
                slot(q, 1)

        @block.scalar
        def _(act):
            for v, a in enumerate((gamma, beta, mean, var)):
                act.dma_start(bn_rows[v:v + 1, :].rearrange("o (a d) -> o a d", a=3),
                              a.unsqueeze(0).unsqueeze(0).to_broadcast([1, 3, CR])).then_inc(bn_rows_in, 16)

            def sums(n, src, total, nm, step):
                for r in range(R):
                    ins = act.activation(unread[0:T, r * C:(r + 1) * C], src[0:T, r * C:(r + 1) * C], ACT.Copy,
                                         accum_out=total[0:T, r:r + 1])
                ins.then_inc(step, 1)
                act.wait_ge(step, 3 * n + 1)
                act.activation(nm[0:T, :], total[0:T, :], ACT.Copy, scale=-1.0 / C).then_inc(step, 1)

            def squares(n, src, nm, sqs, ve, eps, step, ready):
                act.wait_ge(step, 3 * n + 2)
                for r in range(R):
                    ins = act.activation(unread[0:T, r * C:(r + 1) * C], src[0:T, r * C:(r + 1) * C], ACT.Square,
                                         bias=nm[0:T, r:r + 1], accum_out=sqs[0:T, r:r + 1])
                ins.then_inc(step, 1)
                act.wait_ge(step, 3 * n + 3)
                act.activation(ve[0:T, :], sqs[0:T, :], ACT.Copy, scale=1.0 / C, bias=eps).then_inc(ready, 1)

            def sums1(q, bo):
                act.wait_ge(x_in_loaded[bo], 32 * q - 32 * (1 - bo))
                sums(2 * q + bo - 3, x_in[bo], sum1, nm1, ln1_step)

            def squares1(q, bo):
                squares(2 * q + bo - 3, x_in[bo], nm1, sqs1, ve1, LN1_EPS, ln1_step, ve1_ready)

            def sums2(q, bo):
                act.wait_ge(t_done, 2 * q + bo + 1)
                sums(2 * q + bo, t_row, sum2, nm2, ln2_step)

            def squares2(q, bo):
                squares(2 * q + bo, t_row, nm2, sqs2, ve2, LN2_EPS, ln2_step, ve2_ready)

            def apply1(q, bo):
                n = 2 * q + bo
                act.wait_ge(rstd1_ready, n - 2)
                for r in range(R):
                    ins = act.activation(xn[0:T, bass.ds((bo * HP + PAD + r) * C + R * C * q, C)],
                                         x_in[bo][0:T, r * C:(r + 1) * C], ACT.Identity,
                                         bias=nb1[0:T, r:r + 1], scale=rs1[0:T, r:r + 1])
                ins.then_inc(xn_ready, 1)

            def take_xnT(q, bo):
                n = 2 * q + bo
                act.wait_ge(xt_done, n + 1)
                if some(n):
                    act.wait_ge(feat_done, n)
                act.activation(xnT[:, :], misc[:, 0:N], ACT.Copy).then_inc(xnT_ready, 1)

            def features(q, bo):
                n = 2 * q + bo
                act.wait_ge(feat_done, n + 1)
                if some(n - 1):
                    act.wait_ge(kg_ready, STEPS * (n - 1))
                if some(n):
                    act.wait_ge(feat_ready, n)
                act.activation(interior(rT[bo][0:3 * CR, :]),
                               misc[0:3 * CR, 0:N].rearrange("p (r w) -> p r w", w=T),
                               ACT.Relu, bias=bn_bias[:, :], scale=bn_scale[:, :]).then_inc(feat_read, 1)
                act.activation(r_lin[2 * CR:3 * CR, :], misc[2 * CR:3 * CR, 0:N], ACT.Relu,
                               bias=bn_bias[2 * CR:3 * CR, :], scale=bn_scale[2 * CR:3 * CR, :]) \
                    .then_inc(feat_read, 1)

            def take_conv(q, bo):
                n = 2 * q + bo
                act.wait_ge(conv_done, STEPS * (n + 1))
                if some(n):
                    act.wait_ge(back_done, n)
                act.activation(convT[:, :].rearrange("p (r w) -> p r w", w=T),
                               interior(conv_bank[:, 0:R * 2 * WP]), ACT.Copy).then_inc(convT_ready, 1)

            def apply2(q, bo):
                n = 2 * q + bo
                act.wait_ge(rstd2_ready, n + 1)
                if some(n):
                    act.wait_ge(tnT_done, n)
                for r in range(R):
                    ins = act.activation(tn[0:T, r * C:(r + 1) * C], t_row[0:T, r * C:(r + 1) * C], ACT.Identity,
                                         bias=nb2[0:T, r:r + 1], scale=rs2[0:T, r:r + 1])
                ins.then_inc(tn_ready, 1)

            def take_tn_hi(q, bo):
                n = 2 * q + bo
                act.wait_ge(tnT_done, n + 1)
                if some(n - 1):
                    act.wait_ge(h_ready, 2 * E * (n - 1))
                act.activation(tn_hi[bo][:, :], misc[:, 0:N], ACT.Copy).then_inc(tn_hi_ready, 1)

            def take_cwT(q, bo):
                n = 2 * q + bo
                act.wait_ge(cwT_done, n + 1)
                if some(n):
                    act.wait_ge(b2_done, n)
                act.activation(cwT[:, :], misc[0:3 * R * E, 0:T], ACT.Copy).then_inc(cwT_hi_ready, 1)

            def exps(q, bo):
                n = 2 * q + bo
                act.wait_ge(max_ready, n + 1)
                if some(n):
                    act.wait_ge(cw_ready, n)
                for r in range(R):
                    row = slice(r * E, (r + 1) * E)
                    ins = act.activation(ex[0:T, row], neg_logits[0:T, row], ACT.Exp, scale=-1.0,
                                         bias=neg_max[0:T, r:r + 1], accum_out=esum[0:T, r:r + 1])
                ins.then_inc(ex_ready, 1)

            def weigh(q, bo, e):
                m = E * (2 * q + bo) + e
                act.wait_ge(y_done, m + 1)
                if e == 0:
                    act.wait_ge(cw_ready, 2 * q + bo + 1)
                if e != B2_WITH and some(m - 1):
                    act.wait_ge(acc_done, m - 1)
                for r in range(R):
                    rows = slice(r * C, (r + 1) * C)
                    to = y_bank[e % 2] if e == B2_WITH else weighed[e % 2]
                    ins = act.activation(to[0:T, rows], y_bank[e % 2][0:T, rows], ACT.Copy,
                                         scale=cw[bo][0:T, r * E + e:r * E + e + 1])
                ins.then_inc(y_weighed, 1)

            def gelus(q, bo, e):
                m = E * (2 * q + bo) + e
                for f in range(2):
                    act.wait_ge(h_ready, 2 * m + f + 1)
                    if some(m - 1):
                        act.wait_ge(y_done, m - 1)
                    act.activation(hT[e % 2][f][:, :], h_bank[f][:, 0:N], ACT.Gelu,
                                   bias=b1_t[:, 2 * e + f:2 * e + f + 1]).then_inc(gelu_done, 1)

            def slot(q, bo):
                for u in range(STEPS):
                    ql, bl = group(q, bo, 3)
                    qx, bx = group(q, bo, 1)
                    qp, bp = group(q, bo, -1)
                    qg, bg = group(q, bo, -2)
                    if u == 4 and exists(qx):
                        features(qx, bx)
                    if u == 5 and exists(qp):
                        take_tn_hi(qp, bp)
                    if u == 7 and exists(qp):
                        exps(qp, bp)
                    qe, be, e = expert_at(q, bo, u, LAG_WEIGH)
                    if exists(qe):
                        weigh(qe, be, e)
                    qe, be, e = expert_at(q, bo, u, LAG_IN)
                    if exists(qe):
                        gelus(qe, be, e)
                    if u == 0 and exists(qg):
                        take_cwT(qg, bg)
                    if u == 0 and exists(ql):
                        sums1(ql, bl)
                        squares1(ql, bl)
                    if u == 1 and exists(qx):
                        take_xnT(qx, bx)
                    if u == 1 and exists(qp):
                        take_conv(qp, bp)
                    if u == 2 and exists(qp):
                        sums2(qp, bp)
                        squares2(qp, bp)
                    if u == 3 and exists(qp):
                        apply2(qp, bp)
                    if u == 5 and exists(ql):
                        apply1(ql, bl)

            def apply_first(k):
                q, bo = FIRST[k]
                act.wait_ge(first_rstd_ready, k + 1)
                for r in range(R):
                    v = k * R + r
                    ins = act.activation(xn[0:T, ((bo * HP + PAD + r) + R * q) * C:((bo * HP + PAD + r) + R * q + 1) * C],
                                         first_x[k][0:T, r * C:(r + 1) * C], ACT.Identity,
                                         bias=first["nb"][0:T, v:v + 1], scale=first["rs"][0:T, v:v + 1])
                ins.then_inc(xn_ready, 1)

            apply_first(0)
            take_xnT(0, 0)
            apply_first(1)
            act.wait_ge(bn_ready, 2)
            act.wait_ge(pool_const, 20)
            features(0, 0)
            apply_first(2)
            slot(0, 0)
            act.wait_ge(expert_in_sb, 16 * N_EXPERT)
            act.activation(w1_hi[:, :], w1_raw[:, :], ACT.Copy).then_inc(hi_ready, 1)
            act.activation(gate_parts[:, 0:E], gate_raw[:, :], ACT.Copy).then_inc(hi_ready, 1)
            slot(0, 1)
            act.wait_ge(b2_in, 16 * 3 * R)
            act.activation(b2_rows[:, :], b2_raw[:, :], ACT.Copy).then_inc(hi_ready, 1)
            slot(1, 0)
            slot(1, 1)
            with act.Fori(2, QN - 2) as q:
                slot(q, 0)
                slot(q, 1)
            for q in range(QN - 2, QN + 1):
                slot(q, 0)
                slot(q, 1)

        @block.vector
        def _(dve):
            def moments_first(k):
                at = slice(k * R, (k + 1) * R)
                st, both, diff, nm, var_in, sq, ve = (t[0:T, at] for t in (first_st, first_both, *(
                    first[name] for name in ("diff", "nm", "var_in", "sq", "ve"))))
                dve.wait_ge(first_x_loaded[k], 32)
                for r in range(R):
                    ins = dve.bn_stats(st[:, r, :], first_x[k][0:T, r * C:(r + 1) * C])
                ins.then_inc(first_step, 1)
                dve.wait_ge(first_step, 3 * k + 1)
                nc.vector.tensor_tensor(both, st[:, :, 0:3], st[:, :, 3:6], ALU.add)
                nc.vector.tensor_tensor(diff, st[:, :, 1], st[:, :, 4], ALU.subtract).then_inc(first_step, 1)
                dve.wait_ge(first_step, 3 * k + 2)
                dve.tensor_scalar(nm, both[:, :, 1], -0.5, None, ALU.mult)
                dve.tensor_scalar(var_in, both[:, :, 2], 1.0 / C, LN1_EPS, ALU.mult, ALU.add)
                dve.scalar_tensor_tensor(out=sq, in0=diff, scalar=0.25, in1=diff,
                                         op0=ALU.mult, op1=ALU.mult).then_inc(first_step, 1)
                dve.wait_ge(first_step, 3 * k + 3)
                nc.vector.tensor_tensor(ve, var_in, sq, ALU.add).then_inc(first_ve_ready, 1)

            def products(q, bo, u):
                m = STEPS * (2 * q + bo) + u
                r, half = u // 2, u % 2
                jn = JS[half][1]
                if u == 0:
                    qn, _ = group(q, bo, 2)
                    dve.wait_ge(xn_ready, 2 if isinstance(q, int) and q + bo == 0 else
                                2 * q + bo + 3 if exists(qn) else 2 * QN)
                dve.wait_ge(kg_ready, m + 1)
                if some(m - 3):
                    dve.wait_ge(conv_done, m - 3)
                xs = xn[0:T, bass.ds((bo * HP + r) * C + R * C * q, ROWC)]
                xs = xs.rearrange("p (a b) -> p a b", b=CG).unsqueeze(1).to_broadcast([T, jn, K * G, CG])
                ks = kg_bank[half][0:T, 0:jn * K * G].rearrange("p (j a) -> p j a", j=jn)
                ks = ks.unsqueeze(3).to_broadcast([T, jn, K * G, CG])
                po = prod[u % 4][0:T, :].rearrange("p (j a b) -> p j a b", j=jn, b=CG)
                nc.vector.tensor_tensor(po, ks, xs, ALU.mult).then_inc(prod_done, 1)

            def thin(q, bo, u):
                dve.wait_ge(prod_done, STEPS * (2 * q + bo) + u + 1)
                rows = prod[u % 4][0:T, :].rearrange("p (j i) -> p j i", i=ROWC)
                nc.vector.tensor_tensor(rows[:, :, 5 * C:6 * C], rows[:, :, 5 * C:6 * C], rows[:, :, 6 * C:7 * C],
                                        ALU.add).then_inc(thin_done, 1)

            def add_expert(q, bo, e):
                m = E * (2 * q + bo) + e
                dve.wait_ge(y_weighed, m + 1)
                if e == 0 and some(q):
                    dve.wait_ge(out_stored[bo], 32 * q)
                if e == 0:
                    dve.wait_ge(t_done, 2 * q + bo + 1)
                else:
                    dve.wait_ge(acc_done, m)
                if e == B2_WITH:
                    dve.wait_ge(b2_done, 2 * q + bo + 1)
                nc.vector.tensor_tensor(acc[bo][0:T, :], (y_bank if e == B2_WITH else weighed)[e % 2][0:T, :],
                                        (t_row if e == 0 else acc[bo])[0:T, :], ALU.add).then_inc(acc_done, 1)

            def residual(q, bo):
                n = 2 * q + bo
                dve.wait_ge(back_done, n + 1)
                dve.wait_ge(x_res_loaded[bo], 32 * q + 32)
                if some(n):
                    dve.wait_ge(acc_done, E * (n - 1) + 1)
                    dve.wait_ge(tn_ready, n)
                nc.vector.tensor_tensor(t_row[0:T, :], misc[0:T, 0:R * C], x_res[bo][0:T, :], ALU.add) \
                    .then_inc(t_done, 1)

            def take_tn_lo(q, bo):
                dve.wait_ge(tn_hi_ready, 2 * q + bo + 1)
                nc.vector.tensor_tensor(tn_lo[bo][:, :], misc[:, 0:N], tn_hi[bo][:, :].bitcast(F32), ALU.subtract) \
                    .then_inc(tn_lo_ready, 1)

            def take_cwT_lo(q, bo):
                dve.wait_ge(cwT_hi_ready, 2 * q + bo + 1)
                part = slice(R * E, 2 * R * E)
                nc.vector.tensor_tensor(cwT[part, :], misc[part, 0:T], cwT[part, :].bitcast(F32), ALU.subtract) \
                    .then_inc(cwT_ready, 1)

            def per_row(tile):
                return tile[0:T, :].rearrange("p (r e) -> p r e", e=E)

            def spread(tile):
                return tile.to_broadcast([T, R, E])

            SOFT = 8

            def take_logits(q, bo, between):
                n = 2 * q + bo
                dve.wait_ge(gate_done, n + 1)
                parts = misc[0:T, 0:2 * R * E].rearrange("p (r a e) -> p r a e", a=2, e=E)
                nc.vector.tensor_tensor(per_row(logits_part), parts[:, :, 0, :], per_row(gate_bias), ALU.add) \
                    .then_inc(soft_step, 1)
                between()
                dve.wait_ge(soft_step, SOFT * n + 1)
                if some(n):
                    dve.wait_ge(ex_ready, n)
                dve.scalar_tensor_tensor(out=per_row(neg_logits), in0=parts[:, :, 1, :], scalar=-1.0,
                                         in1=per_row(logits_part), op0=ALU.mult, op1=ALU.subtract) \
                    .then_inc(logits_read, 1)
                dve.wait_ge(logits_read, n + 1)
                dve.tensor_reduce(neg_max[0:T, :], per_row(neg_logits), AX.X, ALU.min).then_inc(max_ready, 1)

            def top2_weights(q, bo, between):
                n = 2 * q + bo
                dve.wait_ge(ex_ready, n + 1)
                dve.reciprocal(erec[0:T, :], esum[0:T, :]).then_inc(soft_step, 1)
                for r in range(R):
                    ins = dve.max(top[0:T, r, :], ex[0:T, r * E:(r + 1) * E])
                ins.then_inc(soft_step, 1)
                dve.wait_ge(soft_step, SOFT * n + 3)
                nc.vector.tensor_tensor(per_row(exk), per_row(ex), spread(erec[0:T, :].unsqueeze(2)),
                                        ALU.mult).then_inc(soft_step, 1)
                for r in range(R):
                    ins = dve.max_index(topi[0:T, r, :], top[0:T, r, :], ex[0:T, r * E:(r + 1) * E])
                ins.then_inc(soft_step, 1)
                dve.wait_ge(soft_step, SOFT * n + 5)
                for c, eq in enumerate((eq0, eq1)):
                    nc.vector.tensor_tensor(per_row(eq), per_row(expert_no), spread(topi[0:T, :, c:c + 1]),
                                            ALU.is_equal).then_inc(soft_step, 1)
                between()
                dve.wait_ge(soft_step, SOFT * n + 7)
                nc.vector.tensor_tensor(eqs[0:T, :], eq0[0:T, :], eq1[0:T, :], ALU.add).then_inc(soft_step, 1)
                dve.wait_ge(soft_step, SOFT * n + 8)
                copies = [T, 3, R * E]
                nc.vector.tensor_tensor(cw[bo][0:T, :].rearrange("p (a re) -> p a re", a=3),
                                        exk[0:T, :].unsqueeze(1).to_broadcast(copies),
                                        eqs[0:T, :].unsqueeze(1).to_broadcast(copies), ALU.mult).then_inc(cw_ready, 1)

            def slot(q, bo):
                qg, bg = group(q, bo, -2)
                for u in range(STEPS):
                    qe, be, e = expert_at(q, bo, u, LAG_ADD)
                    if e == B2_WITH and exists(qe):
                        add_expert(qe, be, e)
                    if exists(q):
                        products(q, bo, u)
                    def add_in_turn():
                        if e not in (B2_WITH, E - 1) and exists(qe):
                            add_expert(qe, be, e)

                    qp, bp = group(q, bo, -1)
                    if u < 6 or not exists(qp):
                        add_in_turn()
                    if u in THIN and exists(q) and not plain(q):
                        thin(q, bo, u)
                    if u == 0 and exists(qg):
                        take_cwT_lo(qg, bg)
                    if u == 2 and exists(qp):
                        residual(qp, bp)
                    if u == 5 and exists(qp):
                        take_tn_lo(qp, bp)
                    if u == 6 and exists(qp):
                        take_logits(qp, bp, add_in_turn)
                    if u == 7 and exists(qp):
                        top2_weights(qp, bp, add_in_turn)
                    if u == 7 and exists(qg):
                        add_expert(qg, bg, E - 1)

            moments_first(0)
            dve.wait_ge(bn_turned, 1)
            dve.tensor_copy(bn_in[:, :], kg_bank[1][0:3 * CR, 0:4]).then_inc(bn_step, 1)
            dve.wait_ge(bn_step, 1)
            dve.tensor_scalar(bn_ve[:, :], bn_in[:, 3:4], BN_EPS, None, ALU.add).then_inc(bn_step, 1)
            moments_first(1)
            dve.wait_ge(bn_pow, 1)
            nc.vector.tensor_tensor(bn_scale[:, :], bn_rs[:, :], bn_in[:, 0:1], ALU.mult).then_inc(bn_ready, 1)
            dve.wait_ge(bn_ready, 1)
            nc.vector.tensor_tensor(bn_ms[:, :], bn_scale[:, :], bn_in[:, 2:3], ALU.mult).then_inc(bn_step, 1)
            dve.wait_ge(bn_step, 3)
            nc.vector.tensor_tensor(bn_bias[:, :], bn_in[:, 1:2], bn_ms[:, :], ALU.subtract).then_inc(bn_ready, 1)
            dve.wait_ge(feature_in, 16 * N_FEATURE)
            wk_order = wk_raw.rearrange("p (g i j) -> p j i g", g=G, i=K)
            for j in range(K):
                dve.tensor_copy(wk[:, j * K * G:(j + 1) * K * G].rearrange("p (i g) -> p i g", g=G),
                                wk_order[:, j, :, :]).then_inc(split_step, 1)
            dve.wait_ge(split_step, K)
            for j in range(K):
                part = slice(j * K * G, (j + 1) * K * G)
                ins = nc.vector.tensor_tensor(wk_lo[:, part].rearrange("p (i g) -> p i g", g=G), wk_order[:, j, :, :],
                                              wk[:, part].bitcast(F32).rearrange("p (i g) -> p i g", g=G),
                                              ALU.subtract)
            ins.then_inc(wk_lo_ready, 1)
            dve.wait_ge(wk_lo_ready, 1)
            dve.tensor_copy(wk[CR:2 * CR, :], wk_lo[CR:2 * CR, :].bitcast(F32)).then_inc(split_step, 1)
            moments_first(2)
            dve.wait_ge(split_step, K + 1)
            dve.wait_ge(pool_const, 20)
            slot(0, 0)
            slot(0, 1)
            slot(1, 0)
            slot(1, 1)
            with dve.Fori(2, QN - 2) as q:
                slot(q, 0)
                slot(q, 1)
            for q in range(QN - 2, QN + 1):
                slot(q, 0)
                slot(q, 1)

        @block.tensor
        def _(pe):
            ident_row = ident[0:T, 0:T]

            def transpose_in(q, bo):
                n = 2 * q + bo
                if in_place(q):
                    source, at = xn, (bo * HP + PAD) * C
                    pe.wait_ge(xn_ready, FIRST.index((q, bo)) + 1)
                else:
                    source, at = stage[bo], 0
                    pe.wait_ge(stage_loaded[bo], 16 * q)
                if some(n):
                    pe.wait_ge(feat_read, 2 * n)
                if some(n - 2):
                    pe.wait_ge(cwT_ready, n - 2)
                for r in range(R):
                    mm = pe.transpose(misc[:, r * T:(r + 1) * T], source[0:T, at + r * C:at + (r + 1) * C], ident_row)
                mm.then_inc(xt_done, 1)

            def reduce_channels(q, bo):
                n = 2 * q + bo
                pe.wait_ge(xnT_ready, n + 1)
                if some(n - 1):
                    pe.wait_ge(t_done, n - 1)
                pe.matmul(misc[0:3 * CR, 0:N], wred3[:, :], xnT[:, :], start=True, stop=True) \
                    .then_inc(feat_done, 1)

            def kernels(q, bo, u):
                m = STEPS * (2 * q + bo) + u
                r, half = u // 2, u % 2
                if u == 0:
                    pe.wait_ge(feat_ready, 2 * q + bo + 1)
                if some(m - 1):
                    pe.wait_ge(prod_done, m - 1)
                j0, jn = JS[half]
                for j in range(j0, j0 + jn):
                    mm = pe.matmul(kg_bank[half][0:T, (j - j0) * K * G:(j - j0 + 1) * K * G],
                                   shifted(rT[bo], r, j), wk[:, j * K * G:(j + 1) * K * G],
                                   start=True, stop=True)
                mm.then_inc(kg_ready, 1)

            def gather_taps(q, bo, u):
                m = STEPS * (2 * q + bo) + u
                r, half = u // 2, u % 2
                if plain(q):
                    pe.wait_ge(prod_done, m + 1)
                else:
                    pe.wait_ge(folds_done, m - STEPS * PLAIN + 1)
                if u == 0 and some(2 * q + bo):
                    pe.wait_ge(convT_ready, 2 * q + bo)
                j0, jn = JS[half]
                kept = (list(range(K)) if plain(q) else [0, 2] if u in THIN and u in DEEP
                        else [0, 1, 2] if u in THIN or u in DEEP else [0, 1, 2, 6])
                for j in range(j0, j0 + jn):
                    for i in kept:
                        at = (j - j0) * ROWC + i * C
                        mm = pe.matmul(shifted(conv_bank, r, j), prod[u % 4][0:T, at:at + C],
                                       ident_row, is_transpose=True,
                                       start=(u == 0 and j == j0 and i == 0),
                                       stop=(u == STEPS - 1 and j == K - 1 and i == kept[-1]),
                                       skip_group_check=True)
                mm.then_inc(conv_done, 1)

            def transpose_back(q, bo):
                n = 2 * q + bo
                qx, _ = group(q, bo, 2)
                pe.wait_ge(convT_ready, n + 1)
                if exists(qx):
                    pe.wait_ge(xnT_ready, n + 3)
                else:
                    pe.wait_ge(cwT_ready, n)
                for r in range(R):
                    mm = pe.transpose(misc[0:T, r * C:(r + 1) * C], convT[:, r * T:(r + 1) * T], ident[:, :])
                mm.then_inc(back_done, 1)

            def transpose_tn(q, bo):
                n = 2 * q + bo
                qx, _ = group(q, bo, 2)
                pe.wait_ge(tn_ready, n + 1)
                if exists(qx):
                    pe.wait_ge(feat_read, 2 * n + 6)
                for r in range(R):
                    mm = pe.transpose(misc[:, r * T:(r + 1) * T], tn[0:T, r * C:(r + 1) * C], ident_row)
                mm.then_inc(tnT_done, 1)

            def gate(q, bo):
                pe.wait_ge(tn_lo_ready, 2 * q + bo + 1)
                for r in range(R):
                    at = slice(r * T, (r + 1) * T)
                    first = 2 * r * E
                    pe.matmul(misc[0:T, first:first + 2 * E], tn_hi[bo][:, at], gate_parts[:, :],
                              start=(r == 0), stop=True, skip_group_check=True)
                    mm = pe.matmul(misc[0:T, first:first + E], tn_lo[bo][:, at], gate_parts[:, 0:E],
                                   start=False, stop=True, skip_group_check=True)
                mm.then_inc(gate_done, 1)

            def transpose_cw(q, bo):
                n = 2 * q + bo
                pe.wait_ge(cw_ready, n + 1)
                pe.wait_ge(logits_read, n + 1)
                pe.transpose(misc[0:3 * R * E, 0:T], cw[bo][0:T, :], ident_row).then_inc(cwT_done, 1)

            def expert_bias(q, bo):
                n = 2 * q + bo
                pe.wait_ge(cwT_ready, n + 1)
                pe.wait_ge(y_weighed, E * n + B2_WITH + 1)
                pe.matmul(y_bank[B2_WITH % 2][0:T, 0:R * C], cwT[:, :], b2_rows[:, :], start=False, stop=True,
                          skip_group_check=True).then_inc(b2_done, 1)

            def expert_in(q, bo, e):
                m = E * (2 * q + bo) + e
                if e == 0:
                    pe.wait_ge(tn_lo_ready, 2 * q + bo + 1)
                for f in range(2):
                    if some(m):
                        pe.wait_ge(gelu_done, 2 * m - 1 + f)
                    at = slice(e * HID + f * 128, e * HID + (f + 1) * 128)
                    to = h_bank[f][:, 0:N]
                    pe.matmul(to, w1_hi[:, at], tn_hi[bo][:, :], start=True, stop=False)
                    pe.matmul(to, w1_hi[:, at], tn_lo[bo][:, :], start=False, stop=False)
                    pe.matmul(to, w1_lo[:, at], tn_hi[bo][:, :], start=False, stop=True).then_inc(h_ready, 1)

            def expert_out(q, bo, e):
                m = E * (2 * q + bo) + e
                pe.wait_ge(gelu_done, 2 * m + 2)
                if some(m - 1):
                    pe.wait_ge(y_weighed, m - 1)
                if e == B2_WITH + 2:
                    pe.wait_ge(acc_done, m - 1)
                for r in range(R):
                    for f in range(2):
                        mm = pe.matmul(y_bank[e % 2][0:T, r * C:(r + 1) * C], hT[e % 2][f][:, r * T:(r + 1) * T],
                                       w2_t[:, (2 * e + f) * C:(2 * e + f + 1) * C], start=(r == 0 and f == 0),
                                       stop=(f == 1), skip_group_check=True)
                mm.then_inc(y_done, 1)

            def slot(q, bo):
                qx, bx = group(q, bo, 1)
                qp, bp = group(q, bo, -1)
                qg, bg = group(q, bo, -2)
                for u in range(STEPS):
                    if u == 5 and exists(qp):
                        transpose_tn(qp, bp)
                    if u == 6 and exists(qp):
                        gate(qp, bp)
                    qk, bk = (q, bo) if u < STEPS - 1 else (qx, bx)
                    if exists(qk):
                        kernels(qk, bk, (u + 1) % STEPS)
                    qe, be, e = expert_at(q, bo, u, LAG_IN)
                    if exists(qe):
                        expert_in(qe, be, e)
                    if u == 0 and exists(qg):
                        transpose_cw(qg, bg)
                    if u == 1 and exists(qx):
                        transpose_in(qx, bx)
                    if u == 2 and exists(qp):
                        transpose_back(qp, bp)
                    if u == 3 and exists(qx):
                        reduce_channels(qx, bx)
                    qc, bc = (qp, bp) if u < 2 else (q, bo)
                    if exists(qc):
                        gather_taps(qc, bc, (u - 2) % STEPS)
                    if u == (LAG_WEIGH + B2_WITH) % STEPS and exists(qg):
                        expert_bias(qg, bg)
                    qe, be, e = expert_at(q, bo, u, LAG_OUT)
                    if exists(qe):
                        expert_out(qe, be, e)

            pe.wait_ge(pool_const, 20)
            pe.wait_ge(bn_rows_in, 16 * 4)
            pe.transpose(kg_bank[1][0:3 * CR, 0:4], bn_rows[:, :], ident[0:4, 0:4]).then_inc(bn_turned, 1)
            transpose_in(0, 0)
            pe.wait_ge(feature_in, 16 * N_FEATURE)
            reduce_channels(0, 0)
            pe.wait_ge(split_step, K + 1)
            pe.wait_ge(wk_row_in, 16)
            kernels(0, 0, 0)
            slot(0, 0)
            pe.wait_ge(expert_in_sb, 16 * N_EXPERT)
            pe.wait_ge(experts_split, 2)
            slot(0, 1)
            pe.wait_ge(experts_split, 3)
            slot(1, 0)
            slot(1, 1)
            with pe.Fori(2, QN - 2) as q:
                slot(q, 0)
                slot(q, 1)
            for q in range(QN - 2, QN + 1):
                slot(q, 0)
                slot(q, 1)


_INS = ['x', 'L0_conv_w_reduce', 'L0_conv_gamma', 'L0_conv_beta', 'L0_conv_mean', 'L0_conv_var', 'L0_conv_w_span',
        'L0_conv_b_span', 'L0_ffn_gate_w', 'L0_ffn_gate_b', 'L0_ffn_W1', 'L0_ffn_b1', 'L0_ffn_W2', 'L0_ffn_b2']
_OUTS = [((4, 56, 56, 128), 'float32')]


def kernel(**inputs):
    import numpy as _np
    import concourse.bacc as _bacc
    from concourse import mybir as _mybir
    from concourse.bass_utils import run_bass_kernel_spmd as _run

    nc = _bacc.Bacc("TRN2", target_bir_lowering=False, num_devices=1)
    arrays, args = {}, []
    for name in _INS:
        a = _np.ascontiguousarray(inputs[name])
        arrays[f"in_{name}_dram"] = a
        args.append(nc.dram_tensor(f"in_{name}_dram", a.shape, _mybir.dt.from_np(a.dtype), kind="ExternalInput").ap())
    for i, (shape, dtype) in enumerate(_OUTS):
        dt = _mybir.dt.from_np(_np.dtype(dtype))
        args.append(nc.dram_tensor(f"out_{i}_dram", shape, dt, kind="ExternalOutput").ap())
    metaformer_kernel(nc, *args)
    r = _run(nc, [arrays], core_ids=[0])
    got = tuple(r.results[0][f"out_{i}_dram"] for i in range(len(_OUTS)))
    return got[0]
```
